# Optimizing a Trainium2 kernel written in Bass

```python
import numpy as np
import jax
import jax.numpy as jnp

def _softmax(x, axis=-1):
    return jax.nn.softmax(x, axis=axis)

def _gelu(x):
    return jax.nn.gelu(x, approximate=True)

def _silu(x):
    return jax.nn.silu(x)

def _sigmoid(x):
    return jax.nn.sigmoid(x)

def _layernorm(x, axis=-1, eps=1e-05):
    m = jnp.mean(x, axis=axis, keepdims=True)
    v = jnp.var(x, axis=axis, keepdims=True)
    return (x - m) / jnp.sqrt(v + eps)

def _scatter_add(tgt, idx, src, axis=0):
    return tgt.at[idx].add(src)

def _segment_sum(src, seg, n):
    return jax.ops.segment_sum(src, seg, n)
kernel_name = 'mk_cond_seq_d4_seqx_r8_0cfb96'

def setup_inputs(seed: int=0):
    np.random.seed(seed)
    _w = jnp.asarray

    def _rec_inputs():
        import jax
        import jax.numpy as jnp
        _rk = jax.random.key(seed)
        x = 1.648e-05 + 1 * jax.random.normal(jax.random.fold_in(_rk, 1), (32, 128, 128), jnp.float32)
        _lenS = 128 - jax.random.randint(jax.random.fold_in(_rk, 7), (32,), 0, max(1, 128 // 4) + 1, jnp.int32)
        _lenS2 = 128 - jax.random.randint(jax.random.fold_in(_rk, 8), (32,), 0, max(1, 128 // 4) + 1, jnp.int32)
        cond_1024 = 0.00191187 + 0.999416 * jax.random.normal(jax.random.fold_in(_rk, 11), (32, 128), jnp.float32)
        _validS = jnp.arange(128)[None, :] < _lenS[:, None]
        _validS2 = jnp.arange(128)[None, :] < _lenS2[:, None]
        _causal = jnp.tril(jnp.ones((128, 128), dtype=bool))
        mask_BxSxSx11_ik0 = jnp.where(jnp.ones((32, 128, 128, 11), dtype=bool), 0, 1).astype(jnp.int32)
        return (x, cond_1024, mask_BxSxSx11_ik0)
    x, cond_1024, mask_BxSxSx11_ik0 = _rec_inputs()

    def _L0_cond_setup():
        import jax, jax.numpy as jnp
        import numpy as np
        NONGT = 20
        H = 16
        NEG = -9000000000000000.0

        def _gat_attention(self_feat, cond_adj, label_bias, Wq, bq, Wk, bk, Wout, bout):
            B, N, F = self_feat.shape
            ng = min(NONGT, N)
            dh = F // H
            kv = self_feat[:, :ng]
            qh = (self_feat @ Wq.T + bq).reshape(B, N, H, dh)
            kh = (kv @ Wk.T + bk).reshape(B, ng, H, dh)
            aff = jnp.einsum('bnhd,bmhd->bnhm', qh, kh) * (1.0 / np.sqrt(dh))
            mask = cond_adj[:, :, None, :] > 0
            aff = jnp.where(mask, aff, NEG) + label_bias[:, :, None, :]
            w = jax.nn.softmax(aff, axis=-1)
            out_t = jnp.einsum('bnhm,bmf->bnhf', w, kv)
            out = jnp.einsum('bnhf,hgf->bnhg', out_t, Wout) + bout.reshape(H, F // H)
            return out.reshape(B, N, F)

        def _forward(v, q, adj, W_self, b_self, w_bias, b_bias, Wq, bq, Wk, bk, Wout, bout):
            adj_f = adj.astype(jnp.float32)
            exp_v = v
            row_zero = exp_v.sum(-1) == 0
            q_exp = jnp.where(row_zero[..., None], 0.0, q[:, None, :])
            vcq = jnp.concatenate([exp_v, q_exp], axis=-1)
            self_feat = vcq @ W_self.T + b_self
            output = self_feat
            for d in range(2):
                A = adj_f if d == 0 else jnp.swapaxes(adj_f, 1, 2)
                A = A[:, :, :NONGT, :]
                cond = A.sum(-1)
                vb = A @ w_bias + b_bias
                output = output + _gat_attention(self_feat, cond, vb, Wq[d], bq[d], Wk[d], bk[d], Wout[d], bout[d])
            rel = jax.nn.relu(output)
            return exp_v + rel
        key = jax.random.key(seed)
        ks = jax.random.split(key, 8)
        B, N, L, F, Q = (32, 36, 11, 128, 128)
        IN = F + Q
        s = 0.02
        return {'v': jax.random.normal(ks[0], (B, N, F), jnp.float32), 'q': jax.random.normal(ks[1], (B, Q), jnp.float32), 'adj': jax.random.randint(ks[2], (B, N, N, L), 0, 2, jnp.int32), 'W_self': jax.random.normal(ks[3], (F, IN), jnp.float32) * s, 'b_self': jnp.zeros((F,), jnp.float32), 'w_bias': jax.random.normal(ks[4], (L,), jnp.float32) * s, 'b_bias': jnp.zeros((), jnp.float32), 'Wq': jax.random.normal(ks[5], (2, F, F), jnp.float32) * s, 'bq': jnp.zeros((2, F), jnp.float32), 'Wk': jax.random.normal(ks[6], (2, F, F), jnp.float32) * s, 'bk': jnp.zeros((2, F), jnp.float32), 'Wout': jax.random.normal(ks[7], (2, H, F // H, F), jnp.float32) * s, 'bout': jnp.zeros((2, F), jnp.float32)}
    _L0_cond_all = _L0_cond_setup()
    _L0_cond_in = {k: v for k, v in _L0_cond_all.items() if k in ('W_self', 'b_self', 'w_bias', 'b_bias', 'Wq', 'bq', 'Wk', 'bk', 'Wout', 'bout')}
    del _L0_cond_all

    def _L1_cond_setup():
        import jax, jax.numpy as jnp
        import numpy as np
        D = 128
        H = 16
        HD = 4 * D
        B, T = (4, 128)
        EPS = 1e-05

        def _layernorm(x, g, b):
            mu = jnp.mean(x, axis=-1, keepdims=True)
            var = jnp.mean(jnp.square(x - mu), axis=-1, keepdims=True)
            return (x - mu) * jax.lax.rsqrt(var + EPS) * g + b

        def _attention(x, Wqkv, Wproj, bproj):
            b, t, c = x.shape
            hd = c // H
            qkv = (x @ Wqkv).reshape(b, t, 3, H, hd).transpose(2, 0, 3, 1, 4)
            q, k, v = (qkv[0], qkv[1], qkv[2])
            scale = hd ** (-0.5)
            scores = jnp.einsum('bhqd,bhkd->bhqk', q, k) * scale
            causal = jnp.tril(jnp.ones((t, t), bool))
            scores = jnp.where(causal, scores, -jnp.inf)
            attn = jax.nn.softmax(scores, axis=-1)
            out = jnp.einsum('bhqk,bhkd->bhqd', attn, v)
            out = out.transpose(0, 2, 1, 3).reshape(b, t, c)
            return out @ Wproj + bproj
        key = jax.random.key(seed)
        ks = jax.random.split(key, 12)
        s = 0.02
        return {'x': jax.random.normal(ks[0], (B, T, D), jnp.float32), 'condition': jax.random.normal(ks[1], (B, D), jnp.float32), 'Wqkv': jax.random.normal(ks[2], (D, 3 * D), jnp.float32) * s, 'Wproj': jax.random.normal(ks[3], (D, D), jnp.float32) * s, 'bproj': jnp.zeros((D,), jnp.float32), 'W1': jax.random.normal(ks[4], (D, HD), jnp.float32) * s, 'b1': jnp.zeros((HD,), jnp.float32), 'W2': jax.random.normal(ks[5], (HD, D), jnp.float32) * s, 'b2': jnp.zeros((D,), jnp.float32), 'g1': jnp.ones((D,), jnp.float32), 'be1': jnp.zeros((D,), jnp.float32), 'g2': jnp.ones((D,), jnp.float32), 'be2': jnp.zeros((D,), jnp.float32), 'Wada': jax.random.normal(ks[6], (D, 6 * D), jnp.float32) * s, 'bada': jax.random.normal(ks[7], (6 * D,), jnp.float32) * s}
    _L1_cond_all = _L1_cond_setup()
    _L1_cond_in = {k: v for k, v in _L1_cond_all.items() if k in ('Wqkv', 'Wproj', 'bproj', 'W1', 'b1', 'W2', 'b2', 'g1', 'be1', 'g2', 'be2', 'Wada', 'bada')}
    del _L1_cond_all

    def _L2_cond_setup():
        import jax, jax.numpy as jnp
        import numpy as np
        EPS = 1e-05

        def _sln(h, w, ln_g, ln_b, Wg, bg, Wb, bb):
            mu = jnp.mean(h, axis=-1, keepdims=True)
            var = jnp.mean((h - mu) ** 2, axis=-1, keepdims=True)
            ln = (h - mu) / jnp.sqrt(var + EPS) * ln_g + ln_b
            gamma = (w @ Wg.T + bg)[:, None, :]
            beta = (w @ Wb.T + bb)[:, None, :]
            return gamma * ln + beta
        key = jax.random.key(seed)
        ks = jax.random.split(key, 20)
        B, N, D = (4, 128, 128)
        F = 4 * D
        s = lambda fan: 1.0 / np.sqrt(fan)
        inp = {'hidden': jax.random.normal(ks[0], (B, N, D), jnp.float32), 'w': jax.random.normal(ks[1], (B, D), jnp.float32), 'ln_g': jnp.ones((D,), jnp.float32), 'ln_b': jnp.zeros((D,), jnp.float32), 'Wg': jax.random.normal(ks[2], (D, D), jnp.float32) * s(D), 'bg': jnp.zeros((D,), jnp.float32), 'Wb': jax.random.normal(ks[3], (D, D), jnp.float32) * s(D), 'bb': jnp.zeros((D,), jnp.float32), 'Wqkv': jax.random.normal(ks[4], (3 * D, D), jnp.float32) * s(D), 'bqkv': jnp.zeros((3 * D,), jnp.float32), 'Wp': jax.random.normal(ks[5], (D, D), jnp.float32) * s(D), 'bp': jnp.zeros((D,), jnp.float32), 'W1': jax.random.normal(ks[6], (F, D), jnp.float32) * s(D), 'b1': jnp.zeros((F,), jnp.float32), 'W2': jax.random.normal(ks[7], (D, F), jnp.float32) * s(F), 'b2': jnp.zeros((D,), jnp.float32), 'num_heads': 16}
        return inp
    _L2_cond_all = _L2_cond_setup()
    _L2_cond_in = {k: v for k, v in _L2_cond_all.items() if k in ('ln_g', 'ln_b', 'Wg', 'bg', 'Wb', 'bb', 'Wqkv', 'bqkv', 'Wp', 'bp', 'W1', 'b1', 'W2', 'b2')}
    del _L2_cond_all

    def _L3_cond_setup():
        import jax, jax.numpy as jnp
        import numpy as np
        D = 128
        H = 8
        DH = D // H
        DFF = 512
        EPS = 1e-06

        def _ln(x, g, b):
            mu = jnp.mean(x, axis=-1, keepdims=True)
            var = jnp.mean((x - mu) ** 2, axis=-1, keepdims=True)
            return (x - mu) * jax.lax.rsqrt(var + EPS) * g + b
        key = jax.random.key(seed)
        ks = jax.random.split(key, 16)
        s = 0.02
        return {'x': jax.random.normal(ks[0], (8, 128, D), jnp.float32), 'c': jax.random.normal(ks[1], (8, D), jnp.float32), 'm_ada_w': jax.random.normal(ks[2], (D, 3 * D), jnp.float32) * s, 'm_ada_b': jnp.zeros((3 * D,), jnp.float32), 'm_norm_g': jnp.ones((D,), jnp.float32), 'm_norm_b': jnp.zeros((D,), jnp.float32), 'in_proj_w': jax.random.normal(ks[3], (3 * D, D), jnp.float32) * s, 'in_proj_b': jnp.zeros((3 * D,), jnp.float32), 'out_proj_w': jax.random.normal(ks[4], (D, D), jnp.float32) * s, 'out_proj_b': jnp.zeros((D,), jnp.float32), 'f_ada_w': jax.random.normal(ks[5], (D, 3 * D), jnp.float32) * s, 'f_ada_b': jnp.zeros((3 * D,), jnp.float32), 'f_norm_g': jnp.ones((D,), jnp.float32), 'f_norm_b': jnp.zeros((D,), jnp.float32), 'w1': jax.random.normal(ks[6], (D, DFF), jnp.float32) * s, 'b1': jnp.zeros((DFF,), jnp.float32), 'w2': jax.random.normal(ks[7], (DFF, D), jnp.float32) * s, 'b2': jnp.zeros((D,), jnp.float32)}
    _L3_cond_all = _L3_cond_setup()
    _L3_cond_in = {k: v for k, v in _L3_cond_all.items() if k in ('m_ada_w', 'm_ada_b', 'm_norm_g', 'm_norm_b', 'in_proj_w', 'in_proj_b', 'out_proj_w', 'out_proj_b', 'f_ada_w', 'f_ada_b', 'f_norm_g', 'f_norm_b', 'w1', 'b1', 'w2', 'b2')}
    del _L3_cond_all
    return {'x': x, 'cond_1024': cond_1024, 'mask_BxSxSx11_ik0': mask_BxSxSx11_ik0, 'L0_cond_W_self': _L0_cond_in['W_self'], 'L0_cond_b_self': _L0_cond_in['b_self'], 'L0_cond_w_bias': _L0_cond_in['w_bias'], 'L0_cond_b_bias': _L0_cond_in['b_bias'], 'L0_cond_Wq': _L0_cond_in['Wq'], 'L0_cond_bq': _L0_cond_in['bq'], 'L0_cond_Wk': _L0_cond_in['Wk'], 'L0_cond_bk': _L0_cond_in['bk'], 'L0_cond_Wout': _L0_cond_in['Wout'], 'L0_cond_bout': _L0_cond_in['bout'], 'L1_cond_Wqkv': _L1_cond_in['Wqkv'], 'L1_cond_Wproj': _L1_cond_in['Wproj'], 'L1_cond_bproj': _L1_cond_in['bproj'], 'L1_cond_W1': _L1_cond_in['W1'], 'L1_cond_b1': _L1_cond_in['b1'], 'L1_cond_W2': _L1_cond_in['W2'], 'L1_cond_b2': _L1_cond_in['b2'], 'L1_cond_g1': _L1_cond_in['g1'], 'L1_cond_be1': _L1_cond_in['be1'], 'L1_cond_g2': _L1_cond_in['g2'], 'L1_cond_be2': _L1_cond_in['be2'], 'L1_cond_Wada': _L1_cond_in['Wada'], 'L1_cond_bada': _L1_cond_in['bada'], 'L2_cond_ln_g': _L2_cond_in['ln_g'], 'L2_cond_ln_b': _L2_cond_in['ln_b'], 'L2_cond_Wg': _L2_cond_in['Wg'], 'L2_cond_bg': _L2_cond_in['bg'], 'L2_cond_Wb': _L2_cond_in['Wb'], 'L2_cond_bb': _L2_cond_in['bb'], 'L2_cond_Wqkv': _L2_cond_in['Wqkv'], 'L2_cond_bqkv': _L2_cond_in['bqkv'], 'L2_cond_Wp': _L2_cond_in['Wp'], 'L2_cond_bp': _L2_cond_in['bp'], 'L2_cond_W1': _L2_cond_in['W1'], 'L2_cond_b1': _L2_cond_in['b1'], 'L2_cond_W2': _L2_cond_in['W2'], 'L2_cond_b2': _L2_cond_in['b2'], 'L3_cond_m_ada_w': _L3_cond_in['m_ada_w'], 'L3_cond_m_ada_b': _L3_cond_in['m_ada_b'], 'L3_cond_m_norm_g': _L3_cond_in['m_norm_g'], 'L3_cond_m_norm_b': _L3_cond_in['m_norm_b'], 'L3_cond_in_proj_w': _L3_cond_in['in_proj_w'], 'L3_cond_in_proj_b': _L3_cond_in['in_proj_b'], 'L3_cond_out_proj_w': _L3_cond_in['out_proj_w'], 'L3_cond_out_proj_b': _L3_cond_in['out_proj_b'], 'L3_cond_f_ada_w': _L3_cond_in['f_ada_w'], 'L3_cond_f_ada_b': _L3_cond_in['f_ada_b'], 'L3_cond_f_norm_g': _L3_cond_in['f_norm_g'], 'L3_cond_f_norm_b': _L3_cond_in['f_norm_b'], 'L3_cond_w1': _L3_cond_in['w1'], 'L3_cond_b1': _L3_cond_in['b1'], 'L3_cond_w2': _L3_cond_in['w2'], 'L3_cond_b2': _L3_cond_in['b2']}

def reference(x, cond_1024, mask_BxSxSx11_ik0, L0_cond_W_self, L0_cond_b_self, L0_cond_w_bias, L0_cond_b_bias, L0_cond_Wq, L0_cond_bq, L0_cond_Wk, L0_cond_bk, L0_cond_Wout, L0_cond_bout, L1_cond_Wqkv, L1_cond_Wproj, L1_cond_bproj, L1_cond_W1, L1_cond_b1, L1_cond_W2, L1_cond_b2, L1_cond_g1, L1_cond_be1, L1_cond_g2, L1_cond_be2, L1_cond_Wada, L1_cond_bada, L2_cond_ln_g, L2_cond_ln_b, L2_cond_Wg, L2_cond_bg, L2_cond_Wb, L2_cond_bb, L2_cond_Wqkv, L2_cond_bqkv, L2_cond_Wp, L2_cond_bp, L2_cond_W1, L2_cond_b1, L2_cond_W2, L2_cond_b2, L3_cond_m_ada_w, L3_cond_m_ada_b, L3_cond_m_norm_g, L3_cond_m_norm_b, L3_cond_in_proj_w, L3_cond_in_proj_b, L3_cond_out_proj_w, L3_cond_out_proj_b, L3_cond_f_ada_w, L3_cond_f_ada_b, L3_cond_f_norm_g, L3_cond_f_norm_b, L3_cond_w1, L3_cond_b1, L3_cond_w2, L3_cond_b2):
    import jax
    import jax.numpy as jnp

    def _L0_cond_ref(v, q, adj, W_self, b_self, w_bias, b_bias, Wq, bq, Wk, bk, Wout, bout):
        import jax, jax.numpy as jnp
        import numpy as np
        NONGT = 20
        H = 16
        NEG = -9000000000000000.0

        def _gat_attention(self_feat, cond_adj, label_bias, Wq, bq, Wk, bk, Wout, bout):
            B, N, F = self_feat.shape
            ng = min(NONGT, N)
            dh = F // H
            kv = self_feat[:, :ng]
            qh = (self_feat @ Wq.T + bq).reshape(B, N, H, dh)
            kh = (kv @ Wk.T + bk).reshape(B, ng, H, dh)
            aff = jnp.einsum('bnhd,bmhd->bnhm', qh, kh) * (1.0 / np.sqrt(dh))
            mask = cond_adj[:, :, None, :] > 0
            aff = jnp.where(mask, aff, NEG) + label_bias[:, :, None, :]
            w = jax.nn.softmax(aff, axis=-1)
            out_t = jnp.einsum('bnhm,bmf->bnhf', w, kv)
            out = jnp.einsum('bnhf,hgf->bnhg', out_t, Wout) + bout.reshape(H, F // H)
            return out.reshape(B, N, F)

        def _forward(v, q, adj, W_self, b_self, w_bias, b_bias, Wq, bq, Wk, bk, Wout, bout):
            adj_f = adj.astype(jnp.float32)
            exp_v = v
            row_zero = exp_v.sum(-1) == 0
            q_exp = jnp.where(row_zero[..., None], 0.0, q[:, None, :])
            vcq = jnp.concatenate([exp_v, q_exp], axis=-1)
            self_feat = vcq @ W_self.T + b_self
            output = self_feat
            for d in range(2):
                A = adj_f if d == 0 else jnp.swapaxes(adj_f, 1, 2)
                A = A[:, :, :NONGT, :]
                cond = A.sum(-1)
                vb = A @ w_bias + b_bias
                output = output + _gat_attention(self_feat, cond, vb, Wq[d], bq[d], Wk[d], bk[d], Wout[d], bout[d])
            rel = jax.nn.relu(output)
            return exp_v + rel
        return _forward(v, q, adj, W_self, b_self, w_bias, b_bias, Wq, bq, Wk, bk, Wout, bout)

    def _L1_cond_ref(x, condition, Wqkv, Wproj, bproj, W1, b1, W2, b2, g1, be1, g2, be2, Wada, bada):
        import jax, jax.numpy as jnp
        import numpy as np
        D = 128
        H = 16
        HD = 4 * D
        B, T = (4, 128)
        EPS = 1e-05

        def _layernorm(x, g, b):
            mu = jnp.mean(x, axis=-1, keepdims=True)
            var = jnp.mean(jnp.square(x - mu), axis=-1, keepdims=True)
            return (x - mu) * jax.lax.rsqrt(var + EPS) * g + b

        def _attention(x, Wqkv, Wproj, bproj):
            b, t, c = x.shape
            hd = c // H
            qkv = (x @ Wqkv).reshape(b, t, 3, H, hd).transpose(2, 0, 3, 1, 4)
            q, k, v = (qkv[0], qkv[1], qkv[2])
            scale = hd ** (-0.5)
            scores = jnp.einsum('bhqd,bhkd->bhqk', q, k) * scale
            causal = jnp.tril(jnp.ones((t, t), bool))
            scores = jnp.where(causal, scores, -jnp.inf)
            attn = jax.nn.softmax(scores, axis=-1)
            out = jnp.einsum('bhqk,bhkd->bhqd', attn, v)
            out = out.transpose(0, 2, 1, 3).reshape(b, t, c)
            return out @ Wproj + bproj
        mod = jax.nn.silu(condition) @ Wada + bada
        sh_a, sc_a, gt_a, sh_m, sc_m, gt_m = jnp.split(mod, 6, axis=1)
        xn = _layernorm(x, g1, be1)
        xm = xn * (1.0 + sc_a[:, None, :]) + sh_a[:, None, :]
        x = x + gt_a[:, None, :] * _attention(xm, Wqkv, Wproj, bproj)
        xn = _layernorm(x, g2, be2)
        xm = xn * (1.0 + sc_m[:, None, :]) + sh_m[:, None, :]
        h = jax.nn.gelu(xm @ W1 + b1, approximate=False)
        x = x + gt_m[:, None, :] * (h @ W2 + b2)
        return x

    def _L2_cond_ref(hidden, w, ln_g, ln_b, Wg, bg, Wb, bb, Wqkv, bqkv, Wp, bp, W1, b1, W2, b2, num_heads):
        import jax, jax.numpy as jnp
        import numpy as np
        EPS = 1e-05

        def _sln(h, w, ln_g, ln_b, Wg, bg, Wb, bb):
            mu = jnp.mean(h, axis=-1, keepdims=True)
            var = jnp.mean((h - mu) ** 2, axis=-1, keepdims=True)
            ln = (h - mu) / jnp.sqrt(var + EPS) * ln_g + ln_b
            gamma = (w @ Wg.T + bg)[:, None, :]
            beta = (w @ Wb.T + bb)[:, None, :]
            return gamma * ln + beta
        B, N, D = hidden.shape
        hd = D // num_heads
        h = _sln(hidden, w, ln_g, ln_b, Wg, bg, Wb, bb)
        qkv = (h @ Wqkv.T + bqkv).reshape(B, N, num_heads, hd, 3)
        q = jnp.moveaxis(qkv[..., 0], 2, 1)
        k = jnp.moveaxis(qkv[..., 1], 2, 1)
        v = jnp.moveaxis(qkv[..., 2], 2, 1)
        energy = jnp.einsum('bhqd,bhkd->bhqk', q, k)
        att = jax.nn.softmax(energy, axis=-1) / D ** 0.5
        out = jnp.einsum('bhqk,bhkd->bhqd', att, v)
        out = jnp.moveaxis(out, 1, 2).reshape(B, N, D)
        out = out @ Wp.T + bp
        h1 = out + hidden
        h2 = _sln(h1, w, ln_g, ln_b, Wg, bg, Wb, bb)
        return h2 + h1

    def _L3_cond_ref(x, c, m_ada_w, m_ada_b, m_norm_g, m_norm_b, in_proj_w, in_proj_b, out_proj_w, out_proj_b, f_ada_w, f_ada_b, f_norm_g, f_norm_b, w1, b1, w2, b2):
        import jax, jax.numpy as jnp
        import numpy as np
        D = 128
        H = 8
        DH = D // H
        DFF = 512
        EPS = 1e-06

        def _ln(x, g, b):
            mu = jnp.mean(x, axis=-1, keepdims=True)
            var = jnp.mean((x - mu) ** 2, axis=-1, keepdims=True)
            return (x - mu) * jax.lax.rsqrt(var + EPS) * g + b
        B, N, _ = x.shape
        mod = jax.nn.silu(c) @ m_ada_w + m_ada_b
        shift, scale, gate = jnp.split(mod, 3, axis=-1)
        h = _ln(x, m_norm_g, m_norm_b)
        h = h * (1.0 + scale[:, None, :]) + shift[:, None, :]
        qkv = h @ in_proj_w.T + in_proj_b
        q, k, v = jnp.split(qkv, 3, axis=-1)
        q = q.reshape(B, N, H, DH)
        k = k.reshape(B, N, H, DH)
        v = v.reshape(B, N, H, DH)
        scores = jnp.einsum('bqhd,bkhd->bhqk', q, k) / np.sqrt(DH).astype(np.float32)
        attn = jax.nn.softmax(scores, axis=-1)
        o = jnp.einsum('bhqk,bkhd->bqhd', attn, v).reshape(B, N, D)
        o = o @ out_proj_w.T + out_proj_b
        x = x + gate[:, None, :] * o
        mod2 = jax.nn.silu(c) @ f_ada_w + f_ada_b
        shift2, scale2, gate2 = jnp.split(mod2, 3, axis=-1)
        h = _ln(x, f_norm_g, f_norm_b)
        h = h * (1.0 + scale2[:, None, :]) + shift2[:, None, :]
        h = jax.nn.gelu(h @ w1 + b1, approximate=False) @ w2 + b2
        return x + gate2[:, None, :] * h
    x = _L0_cond_ref(x, cond_1024, mask_BxSxSx11_ik0, L0_cond_W_self, L0_cond_b_self, L0_cond_w_bias, L0_cond_b_bias, L0_cond_Wq, L0_cond_bq, L0_cond_Wk, L0_cond_bk, L0_cond_Wout, L0_cond_bout)
    x = _L1_cond_ref(x, cond_1024, L1_cond_Wqkv, L1_cond_Wproj, L1_cond_bproj, L1_cond_W1, L1_cond_b1, L1_cond_W2, L1_cond_b2, L1_cond_g1, L1_cond_be1, L1_cond_g2, L1_cond_be2, L1_cond_Wada, L1_cond_bada)
    x = _L2_cond_ref(x, cond_1024, L2_cond_ln_g, L2_cond_ln_b, L2_cond_Wg, L2_cond_bg, L2_cond_Wb, L2_cond_bb, L2_cond_Wqkv, L2_cond_bqkv, L2_cond_Wp, L2_cond_bp, L2_cond_W1, L2_cond_b1, L2_cond_W2, L2_cond_b2, 16)
    x = _L3_cond_ref(x, cond_1024, L3_cond_m_ada_w, L3_cond_m_ada_b, L3_cond_m_norm_g, L3_cond_m_norm_b, L3_cond_in_proj_w, L3_cond_in_proj_b, L3_cond_out_proj_w, L3_cond_out_proj_b, L3_cond_f_ada_w, L3_cond_f_ada_b, L3_cond_f_norm_g, L3_cond_f_norm_b, L3_cond_w1, L3_cond_b1, L3_cond_w2, L3_cond_b2)
    return x

_drawn_inputs = setup_inputs


def setup_inputs(seed=0):
    import zlib

    import numpy as np

    out = dict(_drawn_inputs(seed))
    spreads = {'L0_cond_b_self': (0.0, 0.1),
     'L0_cond_bq': (0.0, 0.1),
     'L0_cond_bk': (0.0, 0.1),
     'L0_cond_bout': (0.0, 0.1),
     'L1_cond_bproj': (0.0, 0.765),
     'L1_cond_b1': (0.0, 0.8),
     'L1_cond_b2': (0.0, 0.704),
     'L1_cond_g1': (1.0, 0.6),
     'L1_cond_be1': (0.0, 0.8),
     'L1_cond_g2': (1.0, 0.6),
     'L1_cond_be2': (0.0, 0.8),
     'L2_cond_ln_g': (1.0, 0.2),
     'L2_cond_ln_b': (0.0, 0.271),
     'L2_cond_bg': (0.0, 0.276),
     'L2_cond_bb': (0.0, 0.292),
     'L2_cond_bqkv': (0.0, 2.0),
     'L2_cond_bp': (0.0, 0.296),
     'L2_cond_b1': (0.0, 0.1),
     'L2_cond_b2': (0.0, 0.1),
     'L3_cond_m_ada_b': (0.0, 0.8),
     'L3_cond_m_norm_g': (1.0, 0.6),
     'L3_cond_m_norm_b': (0.0, 0.8),
     'L3_cond_in_proj_b': (0.0, 0.8),
     'L3_cond_out_proj_b': (0.0, 0.8),
     'L3_cond_f_ada_b': (0.0, 0.8),
     'L3_cond_f_norm_g': (1.0, 0.6),
     'L3_cond_f_norm_b': (0.0, 0.8),
     'L3_cond_b1': (0.0, 0.8),
     'L3_cond_b2': (0.0, 0.8)}
    factors = {'L1_cond_Wqkv': 8.0,
     'L1_cond_Wproj': 8.0,
     'L1_cond_W1': 8.0,
     'L1_cond_W2': 8.0,
     'L1_cond_Wada': 3.295,
     'L1_cond_bada': 8.0,
     'L3_cond_m_ada_w': 7.286,
     'L3_cond_in_proj_w': 8.0,
     'L3_cond_out_proj_w': 8.0,
     'L3_cond_f_ada_w': 6.055,
     'L3_cond_w1': 8.0,
     'L3_cond_w2': 8.0}
    for name, (base, spread) in spreads.items():
        noise = np.random.default_rng([zlib.crc32(name.encode()), seed]).standard_normal(out[name].shape)
        drawn = base * np.exp(spread * noise) if base else spread * noise
        out[name] = jnp.asarray(drawn.astype(out[name].dtype))
    for name, factor in factors.items():
        out[name] = (out[name] * factor).astype(out[name].dtype)
    return out
```

```python
import numpy as np
import concourse.bass as bass
from concourse import mybir
from contextlib import ExitStack

B, S, D = 32, 128, 128
GB = 4
NG = B // GB
GT = GB * S
NGT = 20
NL = 11
NEG = 9000000000000000.0

MATS = ["l0_self_x", "l0_self_q", "l0_q0", "l0_q1", "l0_k0", "l0_k1", "l0_out0", "l0_out1",
        "l1_ada0", "l1_ada1", "l1_ada2", "l1_ada3", "l1_ada4", "l1_ada5", "l2_gamma", "l2_beta",
        "l3_m0", "l3_m1", "l3_m2", "l3_f0", "l3_f1", "l3_f2",
        "l1_q", "l1_k", "l1_v", "l1_o",
        "l1_up0", "l1_up1", "l1_up2", "l1_up3", "l1_down0", "l1_down1", "l1_down2", "l1_down3",
        "l2_q", "l2_k", "l2_v", "l2_o",
        "l3_q", "l3_k", "l3_v", "l3_o",
        "l3_up0", "l3_up1", "l3_up2", "l3_up3", "l3_down0", "l3_down1", "l3_down2", "l3_down3"]
N_FIRST = MATS.index("l1_q")
COLS = ["l0_self", "l0_q0", "l0_q1", "l0_k0", "l0_k1",
        "l1_ada0", "l1_ada1", "l1_ada2", "l1_ada3", "l1_ada4", "l1_ada5",
        "l1_g1", "l1_be1", "l1_g2", "l1_be2", "l1_o", "l1_b1_0", "l1_b1_1", "l1_b1_2", "l1_b1_3", "l1_b2",
        "l2_ln_g", "l2_ln_b", "l2_gamma", "l2_beta", "l2_q", "l2_k", "l2_v", "l2_o",
        "l3_m0", "l3_m1", "l3_m2", "l3_f0", "l3_f1", "l3_f2", "l3_g1", "l3_be1", "l3_g2", "l3_be2",
        "l3_q", "l3_k", "l3_v", "l3_o", "l3_b1_0", "l3_b1_1", "l3_b1_2", "l3_b1_3", "l3_b2"]
VECS = ["a1", "c1", "gt1", "gb1", "a2", "c2", "gt2", "gb2", "a3", "c3", "gt3", "gb3",
        "a4", "c4", "gt4", "gb4", "a5", "c5", "gt5", "gb5"]
MI = {n: i for i, n in enumerate(MATS)}
CI = {n: i for i, n in enumerate(COLS)}
VI = {n: i for i, n in enumerate(VECS)}


class Layer:

    def __init__(self, n, name, heads, causal, q_scale, v_scale, ln, gate, biased):
        self.n, self.name, self.heads, self.causal = n, name, heads, causal
        self.q_scale, self.v_scale, self.ln, self.gate, self.biased = q_scale, v_scale, ln, gate, biased
        self.dh = D // heads
        self.halves = heads // 8
        self.half = 128 // self.halves
        self.rows = 6 * self.dh
        self.banks = heads // 4
        self.vw = self.dh + 1


LAYERS = [Layer(0, "l1", 16, True, 8 ** -0.5, 1.0, "1", "1", False),
          Layer(1, "l2", 16, False, 1.0, 128 ** -0.5, "3", "3", True),
          Layer(2, "l3", 8, False, 0.25, 1.0, "4", "4", True)]


class Step:

    def __init__(self, n, s=None, first=0, unroll=1, i=None, t=0):
        self.n, self.fixed, self.first, self.unroll, self.i, self.t = n, s, first, unroll, i, t

    def on(self, lag):
        return self.fixed is None or 0 <= self.fixed - lag < self.n

    def past(self, lag):
        return self.fixed is None or self.fixed - lag >= 0

    def item(self, lag=0):
        if self.fixed is not None:
            return self.fixed - lag
        return self.i * self.unroll + (self.first + self.t - lag)

    def mod(self, lag, m):
        return ((self.fixed if self.fixed is not None else self.first + self.t) - lag) % m

    def div(self, lag, m):
        if self.fixed is not None:
            return (self.fixed - lag) // m
        return self.i * (self.unroll // m) + (self.first + self.t - lag) // m


def run_steps(eng, step, n, last, first, unroll, rounds):
    for s in range(first):
        step(Step(n, s))
    if rounds:
        with eng.Fori(0, rounds) as i:
            for t in range(unroll):
                step(Step(n, None, first, unroll, i, t))
    for s in range(first + unroll * rounds, last):
        step(Step(n, s))


def build(nc, x, cond, adj, mats, cols, rows, out):
    f32, bf16, i32 = mybir.dt.float32, mybir.dt.bfloat16, mybir.dt.int32
    ALU, ACT, AX = mybir.AluOpType, mybir.ActivationFunctionType, mybir.AxisListType

    x_v = x.rearrange("b t f -> t b f")
    out_v = out.rearrange("b t f -> t b f")
    mats_v = mats.rearrange("m i o -> i m o")
    parts_dram = {(l.n, w): nc.dram_tensor(f"parts_{w}_{l.name}", [NG, l.halves, 3, l.half, GT], bf16,
                                           kind="Internal").ap()
                  for l in LAYERS for w in "qk"}
    qv_dram = nc.dram_tensor("query_rows", [B, D], f32, kind="Internal").ap()

    with ExitStack() as ctx:
        def sb(name, shape, dt=f32):
            return ctx.enter_context(nc.sbuf_tensor(name, shape, dt))

        def sem(name):
            return ctx.enter_context(nc.semaphore(name))

        X = sb("X", [128, B, D])
        W = sb("W", [128, len(MATS), 128])
        C = sb("C", [128, len(COLS)])
        V = sb("V", [128, len(VECS), B])
        ident = sb("ident", [128, 128])
        ident_b = sb("ident_b", [128, 128], bf16)
        future = sb("future", [128, 4, 128], bf16)
        future_t = sb("future_t", [128, 4, 128], bf16)
        TQf = sb("TQf", [128, 2 * 8 * GT // 2])
        TKf = sb("TKf", [128, 2 * 8 * GT // 2])
        TQ = TQf[:, :].bitcast(bf16).rearrange("p (r g t) -> p r g t", r=2, g=8)
        TK = TKf[:, :].bitcast(bf16).rearrange("p (r g t) -> p r g t", r=2, g=8)
        self_rows = TQf[:, :].rearrange("p (b f) -> p b f", b=B)
        VALL = sb("VALL", [128, B * 16 * 9])
        PROB = sb("PROB", [128, 2, 16, 128])
        HID = sb("HID", [128, 2, 4, GT])
        STATS = sb("STATS", [128, 2, GB, 6])
        MV = sb("MV", [128, 2, GB, 2])
        VE = sb("VE", [128, 2, GB])
        RSTD = sb("RSTD", [128, 2, GB])
        minus_half = sb("minus_half", [128, GB])
        eps = sb("eps", [128, 2, GB])
        ones = sb("ones", [128, 1])
        after_stats = sb("after_stats", [1, 2])
        XH = sb("XH", [128, 2, GB, D])
        XM = sb("XM", [128, 2, GT])
        QF = sb("QF", [128, GT])
        KF = sb("KF", [128, GT])
        R1 = sb("R1", [128, 2, GT])
        Q3f = sb("Q3f", [128, 3 * GT])
        Q3 = Q3f[:, :].bitcast(bf16).rearrange("p (r c t) -> p r c t", r=2, c=3)
        K3f = sb("K3f", [128, 3 * GT])
        K3 = K3f[:, :].bitcast(bf16).rearrange("p (r c t) -> p r c t", r=2, c=3)
        M = sb("M", [128, 2, 16])
        MB = sb("MB", [128, 2, 32], bf16)
        MT = sb("MT", [32, 2, 128], bf16)
        RD = sb("RD", [128, 2, 16])
        ON = sb("ON", [128, 2, D])
        OT = sb("OT", [128, 2, S])
        YS = sb("YS", [128, 2, S])
        YG = sb("YG", [128, GT])
        O4 = YG
        VS = HID[:, 0, 0:2, :].rearrange("p r (h c) -> p r h c", c=32)
        Q_ROWS = VALL[:, 0:B * D].rearrange("p (b f) -> p b f", b=B)
        WX = HID[:, :, :, :].rearrange("p a b (c d) -> p (a b c) d", d=128)
        WX4 = HID[:, :, :, :].rearrange("p a b (c j m) -> p (a b c) j m", j=GB, m=32)
        WT = PROB[:, :, :, :].rearrange("p a h q -> p (a h) q")
        n0 = GB * NGT * NL
        ADJ0 = TKf[:, 0:n0].bitcast(i32).rearrange("p (b m l) -> p b m l", b=GB, m=NGT)
        ADJ1 = sb("ADJ1", [128, S, NL], i32)
        PR0 = TKf[:, n0:2 * n0].rearrange("p (b m l) -> p b m l", b=GB, m=NGT)
        PR1 = TKf[:, 2 * n0:2 * n0 + S * NL].rearrange("p (t l) -> p t l", l=NL)
        SUM0 = sb("SUM0", [128, 2, GB, NGT])
        SUM1 = sb("SUM1", [128, 2, S])
        ADDN = sb("ADDN", [128, 2, GB, NGT])
        MASK = sb("MASK", [128, B, 2, NGT])
        BIAS = sb("BIAS", [128, B, 2, NGT])
        XS = KF[:, :].rearrange("p (b f) -> p b f", b=GB)
        XSUM = sb("XSUM", [128, GB])
        NZ = sb("NZ", [128, GB])
        QN = QF[:, :].rearrange("p (b f) -> p b f", b=GB)
        XT = XM[:, 0, :]
        SFT = XM[:, 1, :]
        QT0 = XH[:, :, :, :].rearrange("p r b f -> p r (b f)")
        SF32 = sb("SF32", [128, GB * 32])
        KT0 = sb("KT0", [128, 2, GB, NGT])
        head_mask = sb("head_mask", [128, 16, NGT])
        KBLK = sb("KBLK", [128, 2, 2, 16, NGT])
        T0 = Q3f[:, 0:4 * 16 * NGT].rearrange("p (r d h m) -> p r d h m", r=2, d=2, h=16)
        NM0 = sb("NM0", [128, 2, 32])
        V4ALL = sb("V4ALL", [128, NG, 32 * 9])
        V4 = sb("V4", [128, 32, 32])
        HEADS0 = (YG, K3f[:, 0:GT])
        RD0 = sb("RD0", [128, 2, 32])
        O0 = R1[:, 0, :].rearrange("p (r d f) -> p r d f", r=2, d=2)
        U0 = R1[:, 1, 0:2 * D].rearrange("p (r f) -> p r f", r=2)
        w_row = sb("w_row", [128, NL])
        bb_col = sb("bb_col", [128, 1])
        bout_row = sb("bout_row", [128, 2 * D])
        CT = sb("CT", [128, 2, B])
        CR = sb("CR", [B, D])
        EC = sb("EC", [128, 3, B])
        QVS = sb("QVS", [B, D])
        MODS = sb("MODS", [128, 14, B])
        CS = sb("CS", [128, 8])

        P = ctx.enter_context(nc.psum_tensor("P", [128, 8, 512], f32))

        def bank(n, lo=0, hi=512):
            return P[:, n, lo:hi]

        def w(name):
            return W[:, MI[name], :]

        def c(name):
            return C[:, CI[name]:CI[name] + 1]

        def vec(name, b):
            return V[:, VI[name], b]

        s_w = sem("weights_first_in")
        s_w2 = sem("weights_rest_in")
        s_c = sem("columns_in")
        s_cond = sem("condition_in")
        s_rows = sem("row_constants_in")
        s_x = sem("x_first_in")
        s_x2 = sem("x_rest_in")
        s_qvw = sem("query_rows_written")
        s_qvr = sem("query_rows_spread")
        s_set = sem("constants_set")
        s_set1 = sem("constants_cleared")
        s_ct = sem("condition_turned")
        s_cts = sem("condition_copied")
        s_ec = sem("condition_exp")
        s_sl = sem("silu_steps")
        s_mod = sem("modulation_products")
        s_modv = sem("modulation_steps")
        s_qvp = sem("query_product")
        s_qvs = sem("query_product_copied")
        s_cs = sem("scaled_columns")
        a0_in, a1_in = sem("adj_rows_in"), sem("adj_columns_in")
        a_f = sem("adj_as_float")
        a_prod = sem("adj_products")
        a_sum = sem("adj_sums")
        a_t = sem("adj_sums_turned")
        a_n = sem("adj_neg_terms")
        a_used = sem("adj_banks_read")
        xs_in = sem("x_group_in")
        xsum = sem("x_row_sums")
        nz = sem("nonzero_rows")
        qn = sem("query_terms")
        xt0 = sem("x_turned")
        xt0c = sem("x_turned_copied")
        sf0 = sem("self_features")
        sf0c = sem("self_features_copied")
        q0p, q0c = sem("graph_q_products"), sem("graph_q_copied")
        kv0, kv0c = sem("graph_kv_products"), sem("graph_kv_copied")
        sft, sftc = sem("self_rows"), sem("self_rows_copied")
        kblk = sem("graph_key_blocks")
        sc0 = sem("graph_scores")
        t0m, t0b, t0x, t0s, t0e = (sem("graph_masked"), sem("graph_biased"), sem("graph_max"),
                                   sem("graph_shifted"), sem("graph_exp"))
        wt, wtc_a, wtc_v = sem("weights_turned"), sem("weights_copied_act"), sem("weights_copied_dve")
        v4c = sem("graph_values_staged")
        ph0, hc0, ht0 = sem("graph_pv_rows"), sem("graph_heads_copied"), sem("graph_heads_turned")
        pv0, rd0, on0 = sem("graph_pv"), sem("graph_reciprocals"), sem("graph_normalised")
        u0a, u0b = sem("graph_branches_added"), sem("graph_self_added")
        x0 = sem("x_after_graph")
        bst, agg, ve, rs = sem("ln_stats"), sem("ln_moments"), sem("ln_var_eps"), sem("ln_rstd")
        xh, xt, xm = sem("ln_rows"), sem("ln_turned"), sem("ln_modulated")
        qp, kp, vp = sem("q_product"), sem("k_product"), sem("v_product")
        qf, kf, q1, k1, vc = (sem("q_float"), sem("k_float"), sem("q_part1"), sem("k_part1"),
                              sem("v_copied"))
        sp1, sp2, q3, k3 = sem("rest_after_part1"), sem("part2"), sem("q_split"), sem("k_split")
        spk1, spk2 = sem("k_rest_after_part1"), sem("k_part2")
        wrq = [sem(f"q_parts_written{r}") for r in range(2)]
        wrk = [sem(f"k_parts_written{r}") for r in range(2)]
        tl = [sem(f"parts_loaded{r}") for r in range(2)]
        s1, mx = sem("scores_qk"), sem("row_max")
        ms1, ms2 = sem("max_part1"), sem("max_part2")
        mt, mtc = sem("max_turned"), sem("max_copied")
        mrow = [sem(f"max_rows_in{r}") for r in range(2)]
        s2, ex = sem("scores_kq"), sem("exp_done")
        vst, pv, rd, nrm = sem("v_staged"), sem("pv_done"), sem("reciprocals"), sem("normalised")
        ot, otc, yp, yc = sem("o_turned"), sem("o_copied"), sem("y_product"), sem("y_gated")
        yt, xadd = sem("y_turned"), sem("x_after_attention")
        o4c, o4t = sem("heads_out_copied"), sem("heads_out_turned")
        vz = sem("v_padding_cleared")
        ones_k = sem("ones_rows_set")
        ones_v = sem("ones_columns_set")
        up, ge, dn, yg, ygt, xg = (sem("hidden_product"), sem("gelu_done"), sem("down_product"),
                                   sem("mlp_gated"), sem("mlp_turned"), sem("x_after_group"))
        s_out = sem("output_written")

        block = ctx.enter_context(nc.Block())

        LN = [("1", x0, 0, GB), ("2", xadd, 0, GB), ("3", xg, 0, 1), ("3", xadd, B, GB),
              ("4", xg, NG, 1), ("5", xadd, 2 * B, GB)]
        LN_OF = {0: 0, 1: 2, 2: 4}
        G_ROWS, G_TURN, G_MAIN, G_TAIL = 1, 2, 3, 4
        S_MT, S_S2, S_PV, S_NR, S_OT, S_Y, S_YT = 1, 2, 3, 4, 5, 6, 7

        @block.sync
        def _(sp):
            sp.dma_start(CR[:, :], cond).then_inc(s_cond, 16)
            sp.dma_start(C[:, :], cols).then_inc(s_c, 16)
            sp.dma_start(W[:, 0:N_FIRST, :], mats_v[:, 0:N_FIRST, :]).then_inc(s_w, 16)
            sp.dma_start(w_row[:, :], rows[0:NL].partition_broadcast(128)).then_inc(s_rows, 16)
            sp.dma_start(bb_col[:, :], rows[NL:NL + 1].partition_broadcast(128)).then_inc(s_rows, 16)
            sp.dma_start(bout_row[:, :], rows[NL + 1:NL + 1 + 2 * D].partition_broadcast(128)).then_inc(s_rows, 16)

            def load_adj(g):
                if not isinstance(g, int) or g:
                    sp.wait_ge(a_f, 2 * g)
                    sp.wait_ge(a_sum, 4 * g)
                for j in range(GB):
                    sp.dma_start(ADJ0[:, j, :, :], adj[GB * g + j, :, 0:NGT, :]).then_inc(a0_in, 16)
                    sp.dma_start(ADJ1[32 * j:32 * j + NGT, :, :], adj[GB * g + j, 0:NGT, :, :]).then_inc(a1_in, 16)

            def load_xs(g):
                if not isinstance(g, int) or g:
                    sp.wait_ge(xt0, g)
                sp.dma_start(XS[:, :, :], x_v[:, bass.ds(GB * g, GB), :]).then_inc(xs_in, 16)

            load_xs(0)
            sp.dma_start(X[:, 0:GB, :], x_v[:, 0:GB, :]).then_inc(s_x, 16)
            sp.wait_ge(s_set1, 1)
            load_adj(0)
            sp.dma_start(X[:, GB:B, :], x_v[:, GB:B, :]).then_inc(s_x2, 16)
            sp.dma_start(W[:, N_FIRST:, :], mats_v[:, N_FIRST:, :]).then_inc(s_w2, 16)
            sp.wait_ge(s_qvs, 1)
            sp.dma_start(qv_dram, QVS[:, :]).then_inc(s_qvw, 16)
            sp.wait_ge(s_qvw, 16)
            sp.dma_start(Q_ROWS.rearrange("p b f -> p (b f)"),
                         qv_dram.rearrange("b f -> (b f)").partition_broadcast(128)).then_inc(s_qvr, 16)
            with sp.Fori(1, NG) as g:
                load_xs(g)
                load_adj(g)

            for l in LAYERS:
                e_n = l.halves

                def write_parts(st):
                    if not st.on(G_MAIN):
                        return
                    g, r = st.item(G_MAIN), st.mod(G_MAIN, 2)
                    for tile, done, w_, wr in ((Q3, q3, "q", wrq), (K3, k3, "k", wrk)):
                        sp.wait_ge(done, NG * l.n + g + 1)
                        for e in range(e_n):
                            lo = l.half * e
                            dst = parts_dram[l.n, w_][g, e].rearrange("c r t -> r c t")
                            sp.dma_start(dst, tile[lo:lo + l.half, r, :, :]).then_inc(wr[r], 16)

                def load_group(g, r):
                    for e in range(e_n):
                        for tile, w_ in ((TQ, "q"), (TK, "k")):
                            src = parts_dram[l.n, w_][g, e].rearrange("c (d g) t -> (c d) (g t)", g=8)
                            dh, lo = l.dh, l.half * e
                            skip = (0, 1, 2) if w_ == "k" else (0, 0, 0)
                            at = 0
                            for k, n in enumerate((3, 2, 1)):
                                dst = tile[lo + at:lo + at + n * dh, r, :, :].rearrange("p g t -> p (g t)")
                                sp.dma_start(dst, src[skip[k] * dh:(skip[k] + n) * dh, :]).then_inc(tl[r], 16)
                                at += n * dh

                half = NG // 2
                for s in range(half + G_MAIN):
                    write_parts(Step(NG, s))
                sp.wait_ge(wrq[0], WR_BASE[l.n] + 16 * l.halves * half // 2)
                sp.wait_ge(wrk[0], WR_BASE[l.n] + 16 * l.halves * half // 2)
                sp.wait_ge(ones_k, 2 if l.n < 2 else 4)
                if l.n == 0:
                    sp.wait_ge(x0, B)
                else:
                    sp.wait_ge(s2, S2_BASE[l.n])
                load_group(0, 0)
                with sp.Fori(0, half // 2) as i:
                    for t in range(2):
                        write_parts(Step(NG, None, half + G_MAIN, 2, i, t))

                for r in range(2):
                    sp.wait_ge(wrq[r], WR_END[l.n])
                    sp.wait_ge(wrk[r], WR_END[l.n])

                def attend_loads(st):
                    if st.on(S_MT):
                        b = st.item(S_MT)
                        r, u = st.mod(S_MT, 2), st.mod(S_MT, 8)
                        sp.wait_ge(mtc, B * l.n + b + 1)
                        for e in range(e_n):
                            lo = l.half * e + l.rows
                            dst = TQ[lo:lo + 2, u // GB, :, S * (u % GB):S * (u % GB) + S]
                            sp.dma_start(dst, MT[16 * e:16 * e + 16, r, :]).then_inc(mrow[r], 16)
                    if st.mod(0, GB) == S_S2 and (st.fixed is None or st.fixed + GB < B):
                        if st.past(GB):
                            sp.wait_ge(s2, S2_BASE[l.n] + l.banks * GB * st.div(0, GB))
                        load_group(st.div(0, GB) + 1, st.mod(-GB, 8) // GB)

                run_steps(sp, attend_loads, B, B + S_MT, 8, 8, 2)

            with sp.Fori(0, NG) as g:
                sp.wait_ge(xg, 2 * NG + 1 + g)
                sp.dma_start(out_v[:, bass.ds(GB * g, GB), :], X[:, bass.ds(GB * g, GB), :]).then_inc(s_out, 16)
            sp.wait_ge(s_out, 16 * NG)

        @block.gpsimd
        def _(pool):
            pool.memset(ADJ1[:, :, :], 0).then_inc(s_set1, 1)
            pool.memset(ident[:, :], 0.0).then_inc(s_set1, 1)
            pool.memset(ident_b[:, :], 0.0).then_inc(s_set1, 1)
            pool.memset(future[:, :, :], 0.0).then_inc(s_set1, 1)
            pool.memset(future_t[:, :, :], 0.0).then_inc(s_set1, 1)
            pool.memset(head_mask[:, :, :], 1.0).then_inc(s_set1, 1)
            pool.memset(minus_half[:, :], -0.5).then_inc(s_set, 1)
            pool.memset(eps[:, 0, :], 1e-5).then_inc(s_set, 1)
            pool.memset(eps[:, 1, :], 1e-6).then_inc(s_set, 1)
            pool.memset(ones[:, :], 1.0).then_inc(s_set, 1)
            pool.memset(V4ALL[:, :, :], 1.0).then_inc(s_set, 1)
            pool.memset(WX[:, :, :], 0.0).then_inc(s_set, 1)
            pool.memset(V4[:, :, :], 0.0).then_inc(s_set, 1)
            pool.wait_ge(s_set1, 6)
            for m in (ident, ident_b):
                pool.affine_select(out=m[:, :], in_=m[:, :], compare_op=ALU.not_equal, fill=1.0, base=0,
                                   pattern=[[-1, 128]], channel_multiplier=1).then_inc(s_set, 1)
            pool.affine_select(out=future[:, :, :], in_=future[:, :, :], compare_op=ALU.is_ge, fill=-1e30,
                               base=0, pattern=[[0, 4], [-1, 128]], channel_multiplier=1).then_inc(s_set, 1)
            pool.affine_select(out=future_t[:, :, :], in_=future_t[:, :, :], compare_op=ALU.is_ge, fill=-1e30,
                               base=0, pattern=[[0, 4], [1, 128]], channel_multiplier=-1).then_inc(s_set, 1)
            pool.affine_select(out=head_mask[:, :, :], in_=head_mask[:, :, :], compare_op=ALU.is_ge, fill=0.0,
                               base=0, pattern=[[-8, 16], [0, NGT]], channel_multiplier=1).then_inc(s_set1, 1)
            pool.wait_ge(s_set1, 7)
            pool.affine_select(out=head_mask[:, :, :], in_=head_mask[:, :, :], compare_op=ALU.is_ge, fill=0.0,
                               base=7, pattern=[[8, 16], [0, NGT]], channel_multiplier=-1).then_inc(s_set, 1)
            pool.wait_ge(s_rows, 48)
            pool.wait_ge(s_set, 12)

            def adj_products(g):
                pool.wait_ge(a_f, 2 * (g + 1))
                wr = w_row[:, :].unsqueeze(1)
                pool.tensor_tensor(PR0[:, :, :, :].rearrange("p b m l -> p (b m) l"),
                                   PR0[:, :, :, :].rearrange("p b m l -> p (b m) l"),
                                   wr.to_broadcast([128, GB * NGT, NL]), ALU.mult).then_inc(a_prod, 1)
                pool.tensor_tensor(PR1[:, :, :], PR1[:, :, :], wr.to_broadcast([128, S, NL]),
                                   ALU.mult).then_inc(a_prod, 1)

            def query_terms(g):
                pool.wait_ge(nz, g + 1)
                if isinstance(g, int) and g == 0:
                    pool.wait_ge(s_qvr, 16)
                else:
                    pool.wait_ge(sf0, g)
                pool.tensor_tensor(QN[:, :, :], Q_ROWS[:, bass.ds(GB * g, GB), :],
                                   NZ[:, :].unsqueeze(2).to_broadcast([128, GB, D]), ALU.mult).then_inc(qn, 1)

            def key_block(g, j, first):
                pool.wait_ge(kv0c, 3 * (g + 1))
                if not (first and j < 2):
                    pool.wait_ge(sc0, GB * g + j - 1)
                for d in range(2):
                    pool.tensor_tensor(KBLK[:, j % 2, d, :, :],
                                       KT0[:, d, j, :].unsqueeze(1).to_broadcast([128, 16, NGT]),
                                       head_mask[:, :, :], ALU.mult).then_inc(kblk, 1)

            def stage_values(g):
                pool.wait_ge(kv0c, 3 * (g + 1))
                if not (isinstance(g, int) and g == 0):
                    pool.wait_ge(pv0, GB * g)
                pool.tensor_copy(V4[:, :, 0:9], V4ALL[:, g, :].rearrange("p (i c) -> p i c", c=9)).then_inc(v4c, 1)

            def graph_pool(g, first=False, last=False):
                if not first:
                    stage_values(g - 1)
                key_block(g, 0, first)
                for j in range(GB):
                    b = GB * g + j
                    pool.wait_ge(t0m, b + 1)
                    t = T0[:, j % 2, :, :, :]
                    bias = BIAS[:, b, :, :].unsqueeze(2).to_broadcast([128, 2, 16, NGT])
                    pool.tensor_tensor(t, t, bias, ALU.add).then_inc(t0b, 1)
                    if j + 1 < GB:
                        key_block(g, j + 1, first)
                    pool.wait_ge(t0x, b + 1)
                    t = T0[:, j % 2, :, :, :].rearrange("p d h m -> p (d h) m")
                    pool.tensor_tensor(t, t, NM0[:, j % 2, :].unsqueeze(2).to_broadcast([128, 32, NGT]),
                                       ALU.add).then_inc(t0s, 1)
                    if j == 0 and not last:
                        adj_products(g + 1)
                    if j == 1 and not last:
                        query_terms(g + 1)
                    if not first:
                        add_branches(g - 1, j)

            def add_branches(g, j):
                b = GB * g + j
                pool.wait_ge(on0, b + 1)
                if not (isinstance(g, int) and g == 0 and j < 2):
                    pool.wait_ge(x0, b - 1)
                pool.tensor_tensor(U0[:, j % 2, :], O0[:, j % 2, 0, :], O0[:, j % 2, 1, :], ALU.add).then_inc(u0a, 1)
                pool.wait_ge(u0a, b + 1)
                pool.wait_ge(sftc, g + 1)
                pool.tensor_tensor(U0[:, j % 2, :], U0[:, j % 2, :], self_rows[:, b, :], ALU.add).then_inc(u0b, 1)

            adj_products(0)
            query_terms(0)
            graph_pool(0, first=True)
            graph_pool(1)
            with pool.Fori(2, NG - 1) as g:
                graph_pool(g)
            graph_pool(NG - 1, last=True)
            stage_values(NG - 1)
            for j in range(GB):
                add_branches(NG - 1, j)
            pool.memset(TKf[:, :].bitcast(bf16), 1.0).then_inc(ones_k, 2)
            pool.memset(VALL[:, :], 1.0).then_inc(ones_v, 1)

            def ln_rstd(u, st):
                if not st.on(0):
                    return
                g, r = st.item(0), st.mod(0, 2)
                pool.wait_ge(agg, GB * (NG * u + g + 1))
                pool.tensor_tensor(VE[:, r, :], MV[:, r, :, 1], eps[:, 0 if u < 4 else 1, :], ALU.add).then_inc(ve, 1)
                pool.wait_ge(ve, NG * u + g + 1)
                pool.tensor_tensor(RSTD[:, r, :], VE[:, r, :], minus_half[:, :], ALU.pow).then_inc(rs, 1)

            for l in LAYERS:
                u = LN_OF[l.n]

                def project_pool(st):
                    ln_rstd(u, st)
                    if not st.on(G_MAIN):
                        return
                    g, r = st.item(G_MAIN), st.mod(G_MAIN, 2)
                    n = NG * l.n + g
                    pool.wait_ge(qf, n + 1)
                    pool.wait_ge(q1, n + 1)
                    R = R1[:, 0, :]
                    pool.tensor_tensor(R, QF[:, :], Q3[:, r, 0, :], ALU.subtract).then_inc(sp1, 1)
                    pool.wait_ge(sp1, n + 1)
                    pool.tensor_tensor(Q3[:, r, 1, :], R, ones[:, 0:1].to_broadcast([128, GT]),
                                       ALU.mult).then_inc(sp2, 1)
                    pool.wait_ge(sp2, n + 1)
                    pool.tensor_tensor(Q3[:, r, 2, :], R, Q3[:, r, 1, :], ALU.subtract).then_inc(q3, 1)

                if l.n == 2:
                    pool.wait_ge(s2, S2_BASE[2])
                    pool.wait_ge(rs, 4 * NG)
                    pool.memset(TK[96:128, :, :, :], 1.0).then_inc(ones_k, 2)
                    pool.wait_ge(ones_k, 4)
                    pool.memset(VALL[:, :], 1.0).then_inc(ones_v, 1)
                run_steps(pool, project_pool, NG, NG + G_MAIN, 4, 2, 2)

                if l.n == 1:
                    pool.wait_ge(dn, NG)
                pool.wait_ge(rs, NG * (u + 1))
                pool.wait_ge(q3, NG * (l.n + 1))
                pool.wait_ge(k3, NG * (l.n + 1))
                pool.memset(HID[:, 0, 0:2, :], 0.0).then_inc(vz, 1)
                pool.wait_ge(vz, l.n + 1)

                def attend_pool(st):
                    if st.on(S_S2):
                        b, r = st.item(S_S2), st.mod(S_S2, 2)
                        pool.wait_ge(vc, NG * (l.n + 1))
                        if st.past(S_S2 + 2):
                            pool.wait_ge(pv, B * l.n + b - 1)
                        n = l.heads * l.vw
                        pool.tensor_copy(VS[:, r, 0:l.heads, 0:l.vw],
                                         VALL[:, bass.ds(b * n, n)].rearrange("p (h c) -> p h c", c=l.vw))\
                            .then_inc(vst, 1)

                run_steps(pool, attend_pool, B, B + S_S2, 8, 8, 3)
                for u2 in ({0: [1], 1: [3], 2: [5]}[l.n]):
                    run_steps(pool, lambda st: ln_rstd(u2, st), NG, NG, 4, 2, 2)

        @block.scalar
        def _(act):
            act.wait_ge(s_ct, 1)
            act.activation(CT[:, 0, :], bank(0, 0, B), ACT.Copy).then_inc(s_cts, 1)
            act.activation(EC[:, 0, :], bank(0, 0, B), ACT.Exp, scale=-1.0).then_inc(s_ec, 1)
            act.wait_ge(s_qvp, 1)
            act.activation(QVS[:, :], P[0:B, 1, 0:D], ACT.Copy).then_inc(s_qvs, 1)
            act.wait_ge(s_cs, 1)

            def adj_float(g):
                act.wait_ge(a0_in, 64 * (g + 1))
                act.wait_ge(a1_in, 64 * (g + 1))
                if not isinstance(g, int) or g:
                    act.wait_ge(a_sum, 4 * g)
                act.activation(PR0.rearrange("p b m l -> p (b m l)"), ADJ0.rearrange("p b m l -> p (b m l)"),
                               ACT.Copy).then_inc(a_f, 1)
                act.activation(PR1.rearrange("p t l -> p (t l)"), ADJ1[:, :, :].rearrange("p t l -> p (t l)"),
                               ACT.Copy).then_inc(a_f, 1)

            def copy_xt(g):
                act.wait_ge(xt0, g + 1)
                if not isinstance(g, int) or g:
                    act.wait_ge(sf0, g)
                act.activation(XT[:, :], bank(0), ACT.Copy).then_inc(xt0c, 1)

            def copy_sf(g):
                act.wait_ge(sf0, g + 1)
                if not isinstance(g, int) or g:
                    act.wait_ge(sft, g)
                act.activation(SFT[:, :], bank(1), ACT.Identity, bias=c("l0_self")).then_inc(sf0c, 1)
                act.activation(SF32[:, :].rearrange("p (b t) -> p b t", b=GB),
                               bank(1).rearrange("p (b t) -> p b t", b=GB)[:, :, 0:32], ACT.Identity,
                               bias=c("l0_self")).then_inc(sf0c, 1)

            def copy_q(g):
                for d in range(2):
                    act.wait_ge(q0p, 2 * g + d + 1)
                    if not isinstance(g, int) or g:
                        act.wait_ge(sc0, GB * g)
                    act.activation(QT0[:, d, :], bank(2 if d == 0 else 1), ACT.Identity,
                                   bias=CS[:, d:d + 1], scale=8 ** -0.5).then_inc(q0c, 1)

            def exp0(g, j, first):
                b = GB * g + j
                act.wait_ge(t0s, b + 1)
                if not first and j == 0:
                    act.wait_ge(wt, 8 * g)
                act.activation(WX4[:, :, j, 0:NGT], T0[:, j % 2, :, :, :].rearrange("p d h m -> p (d h) m"),
                               ACT.Exp).then_inc(t0e, 1)

            def copy_wt(g):
                for n in range(0, 8, 2):
                    act.wait_ge(wt, 8 * g + n + 1)
                    if n == 0 and not (isinstance(g, int) and g == 0):
                        act.wait_ge(pv0, GB * g)
                    act.activation(WT[:, 4 * n:4 * n + 4, :].rearrange("p i q -> p (i q)"), bank(5),
                                   ACT.Copy).then_inc(wtc_a, 1)

            def copy_heads0(g, j):
                b = GB * g + j
                for d in range(2):
                    act.wait_ge(ph0 if d == 0 else pv0, b + 1)
                    if not (isinstance(g, int) and g == 0 and j == 0):
                        act.wait_ge(ht0, b)
                    act.activation(HEADS0[d][:, :], bank(7), ACT.Copy).then_inc(hc0, 1)

            def graph_act(g, first=False, last=False):
                for j in range(GB):
                    if j == 0 and not first:
                        copy_wt(g - 1)
                    if j == 0 and not last:
                        adj_float(g + 1)
                    if not first:
                        copy_heads0(g - 1, j)
                    exp0(g, j, first)
                    if not last:
                        if j == 1:
                            copy_xt(g + 1)
                        if j == 2:
                            copy_sf(g + 1)
                        if j == 3:
                            copy_q(g + 1)

            act.wait_ge(s_set, 12)
            act.wait_ge(s_c, 16)
            adj_float(0)
            copy_xt(0)
            copy_sf(0)
            copy_q(0)
            graph_act(0, first=True)
            graph_act(1)
            with act.Fori(2, NG - 1) as g:
                graph_act(g)
            graph_act(NG - 1, last=True)
            copy_wt(NG - 1)
            for j in range(GB):
                copy_heads0(NG - 1, j)

            def modulate(u, st):
                if not st.on(G_TURN):
                    return
                g, r = st.item(G_TURN), st.mod(G_TURN, 2)
                act.wait_ge(xt, NG * u + g + 1)
                if st.past(G_TURN + 2):
                    who, base = XM_USED[u]
                    act.wait_ge(who, base + (g - 1) * XM_RISE[u])
                for j in range(GB):
                    b = GB * g + j
                    act.activation(XM[:, r, S * j:S * j + S], bank(r, S * j, S * j + S), ACT.Identity,
                                   bias=V[:, VI["c" + LN[u][0]], bass.ds(b, 1)],
                                   scale=V[:, VI["a" + LN[u][0]], bass.ds(b, 1)]).then_inc(xm, 1)

            XM_USED = {0: (vp, 0), 1: (up, 0), 2: (vp, NG), 3: (ygt, NG), 4: (vp, 2 * NG), 5: (up, 4 * NG)}
            XM_RISE = {0: 1, 1: 4, 2: 1, 3: 1, 4: 1, 5: 4}
            act.wait_ge(s_modv, MODV_END)

            for l in LAYERS:
                u = LN_OF[l.n]

                def project_act(st):
                    modulate(u, st)
                    if not st.on(G_MAIN):
                        return
                    g, r = st.item(G_MAIN), st.mod(G_MAIN, 2)
                    n = NG * l.n + g
                    qb = CS[:, 2 + l.n:3 + l.n] if l.biased else 0.0
                    act.wait_ge(qp, n + 1)
                    if l.n or st.past(G_MAIN + 1):
                        act.wait_ge(q3, n)
                    act.activation(QF[:, :], bank(2 + r), ACT.Identity, bias=qb, scale=l.q_scale).then_inc(qf, 1)
                    if st.past(G_MAIN + 2):
                        act.wait_ge(wrq[r], WR_BASE[l.n] + 16 * l.halves * st.div(G_MAIN, 2))
                    act.activation(Q3[:, r, 0, :], bank(2 + r), ACT.Identity, bias=qb, scale=l.q_scale).then_inc(q1, 1)
                    act.wait_ge(kf, n + 1)
                    if st.past(G_MAIN + 2):
                        act.wait_ge(wrk[r], WR_BASE[l.n] + 16 * l.halves * st.div(G_MAIN, 2))
                    act.activation(K3[:, r, 2, :], KF[:, :], ACT.Copy).then_inc(k1, 1)

                run_steps(act, project_act, NG, NG + G_MAIN, 4 if l.n else 6, 2, 2 if l.n else 1)

                def attend_act(st):
                    def exp_bank(j):
                        if not st.on(S_S2):
                            return
                        b, r = st.item(S_S2), st.mod(S_S2, 2)
                        act.wait_ge(s2, S2_BASE[l.n] + l.banks * b + j + 1)
                        if j == 0 and st.past(S_S2 + 2):
                            act.wait_ge(pv, B * l.n + b - 1)
                        act.activation(PROB[:, r, 4 * j:4 * j + 4, :].rearrange("p h q -> p (h q)"),
                                       bank(2 + j % 2), ACT.Exp).then_inc(ex, 1)

                    def copy_max():
                        if not st.on(S_MT):
                            return
                        b, r = st.item(S_MT), st.mod(S_MT, 2)
                        act.wait_ge(mt, B * l.n + b + 1)
                        if st.past(S_MT + 2):
                            act.wait_ge(mrow[r], MROW_BASE[l.n] + 16 * l.halves * st.div(S_MT, 2))
                        m = 16 * l.halves
                        act.activation(MT[0:m, r, :], P[0:m, 6, 256:320].bitcast(bf16), ACT.Copy).then_inc(mtc, 1)

                    def copy_o():
                        if not st.on(S_OT):
                            return
                        b, r = st.item(S_OT), st.mod(S_OT, 2)
                        act.wait_ge(ot, B * l.n + b + 1)
                        if st.past(S_OT + 2):
                            act.wait_ge(yp, B * l.n + b - 1)
                        vb = {0: 0.0, 1: CS[:, 5:6], 2: c("l3_v")}[l.n]
                        act.activation(OT[:, r, :], bank(6, 0, S), ACT.Identity, bias=vb).then_inc(otc, 1)

                    def gate_y():
                        if not st.on(S_Y):
                            return
                        b, r = st.item(S_Y), st.mod(S_Y, 2)
                        act.wait_ge(yp, B * l.n + b + 1)
                        if st.past(S_Y + 2):
                            act.wait_ge(yt, B * l.n + b - 1)
                        act.activation(YS[:, r, :], bank(7, 0, S), ACT.Identity,
                                       bias=V[:, VI["gb" + l.gate], bass.ds(b, 1)],
                                       scale=V[:, VI["gt" + l.gate], bass.ds(b, 1)]).then_inc(yc, 1)

                    def copy_heads():
                        if not st.on(S_NR):
                            return
                        b = st.item(S_NR)
                        act.wait_ge(pv, B * l.n + b + 1)
                        if st.past(S_NR + 1):
                            act.wait_ge(o4t, B * l.n + b)
                        n = 32 * l.heads
                        act.activation(O4[:, 0:n], bank(4, 0, n), ACT.Copy).then_inc(o4c, 1)

                    copy_heads()
                    if l.banks == 4:
                        exp_bank(0)
                        copy_max()
                        exp_bank(1)
                        copy_o()
                        exp_bank(2)
                        gate_y()
                        exp_bank(3)
                    else:
                        exp_bank(0)
                        copy_max()
                        copy_o()
                        exp_bank(1)
                        gate_y()

                run_steps(act, attend_act, B, B + S_Y, 8, 8, 3)

                if l.n == 1:
                    run_steps(act, lambda st: modulate(3, st), NG, NG + G_TURN, 4, 2, 2)
                    continue
                um, li = (1, 0) if l.n == 0 else (5, 1)
                gate = "2" if l.n == 0 else "5"

                def mlp_act(st):
                    modulate(um, st)
                    if st.on(G_MAIN):
                        g, r = st.item(G_MAIN), st.mod(G_MAIN, 2)
                        for k in range(4):
                            act.wait_ge(up, 4 * (NG * li + g) + k + 1)
                            if k == 0 and st.past(G_MAIN + 2):
                                act.wait_ge(dn, NG * li + g - 1)
                            act.activation(HID[:, r, k, :], bank(2 + k % 2), ACT.Gelu,
                                           bias=c(f"{l.name}_b1_{k}")).then_inc(ge, 1)
                        act.wait_ge(dn, NG * li + g + 1)
                        if st.past(G_MAIN + 1):
                            act.wait_ge(ygt, YGT_BASE[li] + g)
                        for j in range(GB):
                            b = GB * g + j
                            act.activation(YG[:, S * j:S * j + S], bank(4 + r, S * j, S * j + S), ACT.Identity,
                                           bias=V[:, VI["gb" + gate], bass.ds(b, 1)],
                                           scale=V[:, VI["gt" + gate], bass.ds(b, 1)]).then_inc(yg, 1)

                run_steps(act, mlp_act, NG, NG + G_MAIN, 4 if li else 6, 2, 2 if li else 1)

        @block.vector
        def _(dve):
            dve.wait_ge(s_ec, 1)
            dve.tensor_scalar(EC[:, 1, :], EC[:, 0, :], 1.0, None, ALU.add).then_inc(s_sl, 1)
            dve.wait_ge(s_sl, 1)
            dve.reciprocal(EC[:, 2, :], EC[:, 1, :]).then_inc(s_sl, 1)
            dve.wait_ge(s_sl, 2)
            dve.wait_ge(s_cts, 1)
            dve.tensor_tensor(CT[:, 1, :], CT[:, 0, :], EC[:, 2, :], ALU.mult).then_inc(s_sl, 1)
            dve.wait_ge(s_c, 16)
            dve.memset(CS[:, :], 0.0).then_inc(s_sl, 1)
            dve.wait_ge(s_sl, 4)
            for at, name, f in ((0, "l0_q0", 8 ** -0.5), (1, "l0_q1", 8 ** -0.5), (3, "l2_q", 1.0),
                                (4, "l3_q", 0.25), (5, "l2_v", D ** -0.5)):
                last = dve.tensor_scalar(CS[:, at:at + 1], c(name), f, None, ALU.mult)
            last.then_inc(s_cs, 1)
            names = ["l1_ada0", "l1_ada1", "l1_ada2", "l1_ada3", "l1_ada4", "l1_ada5", "l2_gamma", "l2_beta",
                     "l3_m0", "l3_m1", "l3_m2", "l3_f0", "l3_f1", "l3_f2"]
            dve.wait_ge(s_mod, 1)
            for i, name in enumerate(names):
                dve.tensor_scalar(MODS[:, i, :], bank(2, B * i, B * i + B), c(name), None, ALU.add)\
                   .then_inc(s_modv, 1)
            dve.wait_ge(s_modv, len(names))

            def vt(name):
                return V[:, VI[name], :]

            def mod(i):
                return MODS[:, i, :]

            ada = [("1", 1, 0, "l1_g1", "l1_be1"), ("2", 4, 3, "l1_g2", "l1_be2"),
                   ("4", 9, 8, "l3_g1", "l3_be1"), ("5", 12, 11, "l3_g2", "l3_be2")]
            for v_, sc, sh, g_, be in ada:
                dve.tensor_scalar(vt("a" + v_), mod(sc), 1.0, c(g_), ALU.add, ALU.mult).then_inc(s_modv, 1)
                dve.tensor_scalar(vt("c" + v_), mod(sc), 1.0, c(be), ALU.add, ALU.mult).then_inc(s_modv, 1)
            dve.tensor_scalar(vt("a3"), mod(6), c("l2_ln_g"), None, ALU.mult).then_inc(s_modv, 1)
            dve.tensor_scalar(vt("c3"), mod(6), c("l2_ln_b"), None, ALU.mult).then_inc(s_modv, 1)
            dve.memset(vt("gt3"), 1.0).then_inc(s_modv, 1)
            dve.memset(vt("gb3"), 0.0).then_inc(s_modv, 1)
            for v_, gt, bias in (("1", 2, "l1_o"), ("2", 5, "l1_b2"), ("4", 10, "l3_o"), ("5", 13, "l3_b2")):
                dve.tensor_copy(vt("gt" + v_), mod(gt)).then_inc(s_modv, 1)
                dve.tensor_scalar(vt("gb" + v_), mod(gt), c(bias), None, ALU.mult).then_inc(s_modv, 1)
            dve.wait_ge(s_modv, 34)
            for v_, sc, sh, g_, be in ada:
                dve.tensor_tensor(vt("c" + v_), vt("c" + v_), mod(sh), ALU.add).then_inc(s_modv, 1)
            dve.tensor_tensor(vt("c3"), vt("c3"), mod(7), ALU.add).then_inc(s_modv, 1)
            dve.tensor_scalar(vt("gb3"), vt("gb3"), c("l2_o"), None, ALU.add).then_inc(s_modv, 1)

            def adj_sums(g):
                dve.wait_ge(a0_in, 64 * (g + 1))
                dve.wait_ge(a1_in, 64 * (g + 1))
                if not isinstance(g, int) or g:
                    dve.wait_ge(a_t, g)
                    dve.wait_ge(a_used, 4 * g)
                dve.tensor_reduce(SUM0[:, 0, :, :].rearrange("p b m -> p (b m)"),
                                  ADJ0[:, :, :, :].rearrange("p b m l -> p (b m) l"), AX.X, ALU.add).then_inc(a_sum, 1)
                dve.tensor_reduce(SUM1[:, 0, :], ADJ1[:, :, :], AX.X, ALU.add).then_inc(a_sum, 1)

            def adj_sums2(g):
                dve.wait_ge(a_prod, 2 * (g + 1))
                dve.tensor_reduce(SUM0[:, 1, :, :].rearrange("p b m -> p (b m)"),
                                  PR0[:, :, :, :].rearrange("p b m l -> p (b m) l"), AX.X, ALU.add).then_inc(a_sum, 1)
                dve.tensor_reduce(SUM1[:, 1, :], PR1[:, :, :], AX.X, ALU.add).then_inc(a_sum, 1)

            def adj_masks(g):
                dve.wait_ge(a_t, g + 1)
                dve.wait_ge(a_sum, 4 * (g + 1))
                turned = P[:, 2, 0:256].rearrange("p (s j m) -> p s j m", s=2, j=GB)
                for d in range(2):
                    cnt = SUM0[:, 0, :, :] if d == 0 else turned[:, 0, :, 0:NGT]
                    val = SUM0[:, 1, :, :] if d == 0 else turned[:, 1, :, 0:NGT]
                    mk = MASK[:, bass.ds(GB * g, GB), d, :]
                    dve.tensor_scalar(mk, cnt, 0.0, None, ALU.is_gt).then_inc(a_n, 1)
                    dve.wait_ge(a_n, 4 * g + 2 * d + 1)
                    dve.tensor_scalar(ADDN[:, d, :, :], mk, NEG, -NEG, ALU.mult, ALU.add).then_inc(a_n, 1)
                    dve.wait_ge(a_n, 4 * g + 2 * d + 2)
                    dve.scalar_tensor_tensor(out=BIAS[:, bass.ds(GB * g, GB), d, :], in0=val, scalar=bb_col[:, 0:1],
                                             in1=ADDN[:, d, :, :], op0=ALU.add, op1=ALU.add).then_inc(a_used, 2)

            def nonzero(g, first):
                dve.wait_ge(s_x if first else s_x2, 16)
                if not first:
                    dve.wait_ge(qn, g)
                dve.tensor_reduce(XSUM[:, :], X[:, bass.ds(GB * g, GB), :], AX.X, ALU.add).then_inc(xsum, 1)
                dve.wait_ge(xsum, g + 1)
                dve.tensor_scalar(NZ[:, :], XSUM[:, :], 0.0, None, ALU.not_equal).then_inc(nz, 1)

            def copy_kv(g, first):
                dve.wait_ge(kv0, g + 1)
                if not first:
                    dve.wait_ge(kblk, 8 * g)
                for d in range(2):
                    dve.tensor_scalar(KT0[:, d, :, :].rearrange("p b m -> p (b m)"), bank(0, 80 * d, 80 * d + 80),
                                      c(f"l0_k{d}"), None, ALU.add).then_inc(kv0c, 1)
                v4 = V4ALL[:, g, :].rearrange("p (i c) -> p i c", c=9)[:, :, 0:8]
                dve.tensor_tensor(v4, bank(0, 256, 512).rearrange("p (i c) -> p i c", c=8),
                                  bout_row[:, :].rearrange("p (i c) -> p i c", c=8), ALU.add).then_inc(kv0c, 1)

            def copy_self(g):
                dve.wait_ge(sft, g + 1)
                dve.tensor_copy(self_rows[:, bass.ds(GB * g, GB), :].rearrange("p b f -> p (b f)"), bank(0))\
                   .then_inc(sftc, 1)

            def scores0(g, j, first):
                b = GB * g + j
                dve.wait_ge(sc0, b + 1)
                if not (first and j < 2):
                    dve.wait_ge(t0e, b - 1)
                mk = MASK[:, b, :, :].unsqueeze(2).to_broadcast([128, 2, 16, NGT])
                dve.tensor_tensor(T0[:, j % 2, :, :, :],
                                  P[:, 3:5, 0:320].rearrange("p d (h m) -> p d h m", m=NGT), mk,
                                  ALU.mult).then_inc(t0m, 1)

            def max0(g, j):
                b = GB * g + j
                dve.wait_ge(t0b, b + 1)
                dve.tensor_reduce(NM0[:, j % 2, :], T0[:, j % 2, :, :, :].rearrange("p d h m -> p (d h) m"),
                                  AX.X, ALU.max, negate=True).then_inc(t0x, 1)

            def copy_wt_dve(g):
                for n in range(1, 8, 2):
                    dve.wait_ge(wt, 8 * g + n + 1)
                    if n == 1 and not (isinstance(g, int) and g == 0):
                        dve.wait_ge(pv0, GB * g)
                    dve.tensor_copy(WT[:, 4 * n:4 * n + 4, :].rearrange("p i q -> p (i q)"), bank(6))\
                       .then_inc(wtc_v, 1)

            def normalise0(g, j):
                b = GB * g + j
                o = P[:, 5:7, :].rearrange("p a (i c) -> p (a i) c", c=32)
                dve.wait_ge(ht0, b + 1)
                dve.reciprocal(RD0[:, j % 2, :].unsqueeze(2), o[:, :, 8:9]).then_inc(rd0, 1)
                dve.wait_ge(rd0, b + 1)
                if not (isinstance(g, int) and g == 0 and j < 2):
                    dve.wait_ge(u0a, b - 1)
                dve.tensor_tensor(O0[:, j % 2, :, :].rearrange("p d (h c) -> p (d h) c", c=8), o[:, :, 0:8],
                                  RD0[:, j % 2, :].unsqueeze(2).to_broadcast([128, 32, 8]), ALU.mult).then_inc(on0, 1)

            def finish0(g, j):
                b = GB * g + j
                dve.wait_ge(u0b, b + 1)
                dve.scalar_tensor_tensor(out=X[:, b, :], in0=U0[:, j % 2, :], scalar=0.0, in1=X[:, b, :],
                                         op0=ALU.max, op1=ALU.add).then_inc(x0, 1)

            def graph_dve(g, first=False, last=False):
                for j in range(GB):
                    scores0(g, j, first)
                    if j == 0 and not first:
                        copy_wt_dve(g - 1)
                    if j == 0 and not last:
                        nonzero(g + 1, False)
                        adj_sums(g + 1)
                    if j == 1 and not last:
                        adj_sums2(g + 1)
                    if j == 2 and not last:
                        adj_masks(g + 1)
                    max0(g, j)
                    if j == 3 and not last:
                        copy_kv(g + 1, False)
                        copy_self(g + 1)
                    if not first:
                        normalise0(g - 1, j)
                        finish0(g - 1, j)

            dve.wait_ge(s_rows, 48)
            dve.wait_ge(s_set, 12)
            nonzero(0, True)
            adj_sums(0)
            adj_sums2(0)
            adj_masks(0)
            copy_kv(0, True)
            copy_self(0)
            graph_dve(0, first=True)
            graph_dve(1)
            with dve.Fori(2, NG - 1) as g:
                graph_dve(g)
            graph_dve(NG - 1, last=True)
            copy_wt_dve(NG - 1)
            for j in range(GB):
                normalise0(NG - 1, j)
                finish0(NG - 1, j)

            def ln_rows(u, st):
                _, ready, base, rise = LN[u]
                if st.on(0):
                    g, r = st.item(0), st.mod(0, 2)
                    n = NG * u + g
                    dve.wait_ge(ready, base + rise * (g + 1))
                    if u or st.past(2):
                        dve.wait_ge(ve, n - 1)
                    for j in range(GB):
                        dve.bn_stats(STATS[:, r, j, :], X[:, GB * g + j, :]).then_inc(bst, 1)
                    dve.wait_ge(bst, GB * (n + 1))
                    dve.memset(after_stats[:, r:r + 1], 0.0)
                    for j in range(GB):
                        dve.bn_aggr(MV[:, r, j, :], STATS[:, r, j, :]).then_inc(agg, 1)
                if st.on(G_ROWS):
                    g, r = st.item(G_ROWS), st.mod(G_ROWS, 2)
                    n = NG * u + g
                    dve.wait_ge(rs, n + 1)
                    if u or st.past(G_ROWS + 2):
                        dve.wait_ge(xt, n - 1)
                    for j in range(GB):
                        dve.tensor_scalar(XH[:, r, j, :], X[:, GB * g + j, :], MV[:, r, j, 0:1],
                                          RSTD[:, r, j:j + 1], ALU.subtract, ALU.mult).then_inc(xh, 1)

            for l in LAYERS:
                u = LN_OF[l.n]
                if l.n != 1:
                    dve.wait_ge(ones_v, 1 if l.n == 0 else 2)

                def project_dve(st):
                    ln_rows(u, st)
                    if not st.on(G_MAIN):
                        return
                    g, r = st.item(G_MAIN), st.mod(G_MAIN, 2)
                    n = NG * l.n + g
                    dve.wait_ge(kp, n + 1)
                    if l.n or st.past(G_MAIN + 1):
                        dve.wait_ge(k3, n)
                    kb = c(l.name + "_k") if l.biased else 0.0
                    dve.tensor_scalar(KF[:, :], bank(4 + r), kb, None, ALU.add).then_inc(kf, 1)
                    dve.wait_ge(vp, n + 1)
                    w_ = l.heads * l.vw
                    dst = VALL[:, bass.ds(GB * w_ * g, GB * w_)].rearrange("p (h c) -> p h c", c=l.vw)[:, :, 0:l.dh]
                    dve.tensor_scalar(dst, bank(6 + r).rearrange("p (h c) -> p h c", c=l.dh), l.v_scale, None,
                                      ALU.mult).then_inc(vc, 1)
                    dve.wait_ge(k1, n + 1)
                    R = R1[:, 1, :]
                    dve.tensor_tensor(R, KF[:, :], K3[:, r, 2, :], ALU.subtract).then_inc(spk1, 1)
                    dve.wait_ge(spk1, n + 1)
                    dve.tensor_copy(K3[:, r, 1, :], R).then_inc(spk2, 1)
                    dve.wait_ge(spk2, n + 1)
                    dve.tensor_tensor(K3[:, r, 0, :], R, K3[:, r, 1, :], ALU.subtract).then_inc(k3, 1)

                run_steps(dve, project_dve, NG, NG + G_MAIN, 4, 2, 2)

                def attend_dve(st):
                    def max_bank(j):
                        if not st.on(0):
                            return
                        b, r = st.item(0), st.mod(0, 2)
                        dve.wait_ge(s1, S2_BASE[l.n] + l.banks * b + j + 1)
                        if j == 0 and st.past(2):
                            dve.wait_ge(ms2, B * l.n + b - 1)
                        dve.tensor_reduce(M[:, r, 4 * j:4 * j + 4], bank(j % 2).rearrange("p (h k) -> p h k", h=4),
                                          AX.X, ALU.max, negate=True).then_inc(mx, 1)

                    def split_max():
                        if not st.on(0):
                            return
                        b, r = st.item(0), st.mod(0, 2)
                        m = M[:, r, 0:l.heads].rearrange("p (e g) -> p e g", g=8)
                        parts = MB[:, r, 0:2 * l.heads].rearrange("p (e c g) -> p e c g", c=2, g=8)
                        dve.wait_ge(mx, S2_BASE[l.n] + l.banks * (b + 1))
                        if st.past(2):
                            dve.wait_ge(mt, B * l.n + b - 1)
                        dve.tensor_copy(parts[:, :, 0, :], m).then_inc(ms1, 1)
                        dve.wait_ge(ms1, B * l.n + b + 1)
                        dve.tensor_tensor(parts[:, :, 1, :], m, parts[:, :, 0, :], ALU.subtract).then_inc(ms2, 1)

                    def normalise():
                        if not st.on(S_NR):
                            return
                        b, r = st.item(S_NR), st.mod(S_NR, 2)
                        o = P[:, 5, 0:32 * l.heads].rearrange("p (h c) -> p h c", c=32)
                        dve.wait_ge(o4t, B * l.n + b + 1)
                        dve.reciprocal(RD[:, r, 0:l.heads].unsqueeze(2), o[:, :, l.dh:l.vw]).then_inc(rd, 1)
                        dve.wait_ge(rd, B * l.n + b + 1)
                        if st.past(S_NR + 2):
                            dve.wait_ge(ot, B * l.n + b - 1)
                        dve.tensor_tensor(ON[:, r, :].rearrange("p (h c) -> p h c", c=l.dh), o[:, :, 0:l.dh],
                                          RD[:, r, 0:l.heads].unsqueeze(2).to_broadcast([128, l.heads, l.dh]),
                                          ALU.mult).then_inc(nrm, 1)

                    def add_x():
                        if not st.on(S_YT):
                            return
                        b = st.item(S_YT)
                        dve.wait_ge(yt, B * l.n + b + 1)
                        dve.tensor_tensor(X[:, b, :], bank(7, 0, D), X[:, b, :], ALU.add).then_inc(xadd, 1)

                    for j in range(l.banks):
                        max_bank(j)
                    split_max()
                    add_x()
                    normalise()

                run_steps(dve, attend_dve, B, B + S_YT, 8, 8, 3)

                um = {0: 1, 1: 3, 2: 5}[l.n]

                def group_tail(st):
                    ln_rows(um, st)
                    if st.on(G_TAIL):
                        g, r = st.item(G_TAIL), st.mod(G_TAIL, 2)
                        dve.wait_ge(ygt, NG * l.n + g + 1)
                        xs = X[:, bass.ds(GB * g, GB), :].rearrange("p b f -> p (b f)")
                        dve.tensor_tensor(xs, bank(6 + r), xs, ALU.add).then_inc(xg, 1)

                run_steps(dve, group_tail, NG, NG + G_TAIL, 4, 2, 2)

        @block.tensor
        def _(pe):
            pe.wait_ge(s_set, 12)
            pe.wait_ge(s_cond, 16)
            pe.transpose(bank(0, 0, B), CR[:, :], ident[0:B, 0:B]).then_inc(s_ct, 1)
            pe.wait_ge(s_w, 16)
            pe.wait_ge(s_cts, 1)
            pe.matmul(P[0:B, 1, 0:D], CT[:, 0, :], w("l0_self_q"), start=True, stop=True).then_inc(s_qvp, 1)
            pe.wait_ge(s_sl, 3)
            names = ["l1_ada0", "l1_ada1", "l1_ada2", "l1_ada3", "l1_ada4", "l1_ada5", "l2_gamma", "l2_beta",
                     "l3_m0", "l3_m1", "l3_m2", "l3_f0", "l3_f1", "l3_f2"]
            for i, name in enumerate(names):
                last = pe.matmul(bank(2, B * i, B * i + B), w(name), CT[:, 0 if name[:2] == "l2" else 1, :],
                                 start=True, stop=True)
            last.then_inc(s_mod, 1)
            pe.wait_ge(s_ec, 1)
            pe.wait_ge(s_qvs, 1)
            pe.wait_ge(s_modv, len(names))

            def turn_x(g, first):
                pe.wait_ge(xs_in, 16 * (g + 1))
                if not first:
                    pe.wait_ge(sftc, g)
                for j in range(GB):
                    last = pe.transpose(bank(0, S * j, S * j + S), XS[:, j, :], ident[:, :])
                last.then_inc(xt0, 1)

            def self_features(g, first):
                pe.wait_ge(xt0c, g + 1)
                pe.wait_ge(qn, g + 1)
                if not first:
                    pe.wait_ge(q0c, 2 * g)
                pe.matmul(bank(1), w("l0_self_x"), XT[:, :], start=True, stop=False, skip_group_check=True)
                for j in range(GB):
                    last = pe.matmul(bank(1, S * j, S * j + S), QN[:, j, :], ident[:, :], start=False,
                                     stop=(j == GB - 1), skip_group_check=True)
                last.then_inc(sf0, 1)

            def turn_adj(g, first):
                pe.wait_ge(a_sum, 4 * (g + 1))
                if not first:
                    pe.wait_ge(q0c, 2 * g)
                for i in range(2):
                    last = pe.transpose(bank(2, 128 * i, 128 * i + 128), SUM1[:, i, :], ident[:, :])
                last.then_inc(a_t, 1)

            def graph_products(g):
                pe.wait_ge(sf0c, 2 * (g + 1))
                pe.wait_ge(a_used, 4 * (g + 1))
                pe.matmul(bank(2), w("l0_q0"), SFT[:, :], start=True, stop=True).then_inc(q0p, 1)
                pe.matmul(bank(1), w("l0_q1"), SFT[:, :], start=True, stop=True).then_inc(q0p, 1)
                sf = SFT[:, :].rearrange("p (b t) -> p b t", b=GB)
                for d in range(2):
                    pe.matmul(bank(0, 80 * d, 80 * d + 80), w(f"l0_k{d}"), sf[:, :, 0:NGT], start=True, stop=True)
                pe.matmul(bank(0, 256, 512), SF32[:, :],
                          W[:, MI["l0_out0"]:MI["l0_out0"] + 2, :].rearrange("p a n -> p (a n)"),
                          start=True, stop=True).then_inc(kv0, 1)
                pe.wait_ge(kv0c, 3 * (g + 1))
                for j in range(GB):
                    last = pe.transpose(bank(0, S * j, S * j + S), SFT[:, S * j:S * j + S], ident[:, :])
                last.then_inc(sft, 1)

            def graph_scores(g, j, first):
                b = GB * g + j
                if j == 0:
                    pe.wait_ge(q0c, 2 * (g + 1))
                pe.wait_ge(kblk, 2 * (b + 1))
                if not (first and j == 0):
                    pe.wait_ge(t0m, b)
                for d in range(2):
                    last = pe.matmul(P[:, 3 + d, 0:320], QT0[:, d, S * j:S * j + S],
                                     KBLK[:, j % 2, d, :, :].rearrange("p h m -> p (h m)"), start=True, stop=True)
                last.then_inc(sc0, 1)

            def turn_weights(g):
                pe.wait_ge(t0e, GB * (g + 1))
                if not (isinstance(g, int) and g == 0):
                    pe.wait_ge(on0, GB * g)
                for n in range(8):
                    if n >= 2 or not (isinstance(g, int) and g == 0):
                        done = wtc_a if n % 2 == 0 else wtc_v
                        pe.wait_ge(done, 4 * g + n // 2)
                    for i in range(4):
                        last = pe.transpose(bank(5 + n % 2, 128 * i, 128 * i + 128), WX[:, 4 * n + i, :], ident[:, :])
                    last.then_inc(wt, 1)

            def graph_pv(g, j):
                b = GB * g + j
                if j == 0:
                    pe.wait_ge(wtc_a, 4 * (g + 1))
                    pe.wait_ge(wtc_v, 4 * (g + 1))
                    pe.wait_ge(v4c, g + 1)
                lo = 32 * j
                for d in range(2):
                    if not (isinstance(g, int) and g == 0 and j == 0 and d == 0):
                        pe.wait_ge(hc0, 2 * b + d)
                    for h in range(16):
                        i, at, n = 16 * d + h, 32 * (h % 4), 2 if h == 0 else 1
                        last = pe.matmul(P[at:at + 32 * n, 7, 128 * (h // 4):128 * (h // 4) + 128],
                                         V4[lo:lo + NGT, i:i + n, :].rearrange("p h c -> p (h c)"),
                                         WT[lo:lo + NGT, i, :], start=True, stop=True,
                                         tile_position=(lo, at))
                    last.then_inc(ph0 if d == 0 else pv0, 1)
                for d in range(2):
                    pe.wait_ge(hc0, 2 * b + d + 1)
                    if d == 0 and not (isinstance(g, int) and g == 0 and j == 0):
                        pe.wait_ge(on0, b)
                    for i in range(4):
                        last = pe.transpose(bank(5 + d, 128 * i, 128 * i + 128),
                                            HEADS0[d][:, 128 * i:128 * i + 128], ident[:, :])
                last.then_inc(ht0, 1)

            def graph_pe(g, first=False, last=False):
                for j in range(GB):
                    graph_scores(g, j, first)
                    if j == 0 and not first:
                        turn_weights(g - 1)
                    if not first:
                        graph_pv(g - 1, j)
                    if not last:
                        if j == 1:
                            turn_x(g + 1, False)
                        if j == 2:
                            turn_adj(g + 1, False)
                            self_features(g + 1, False)
                        if j == 3:
                            graph_products(g + 1)

            turn_x(0, True)
            turn_adj(0, True)
            self_features(0, True)
            graph_products(0)
            graph_pe(0, first=True)
            graph_pe(1)
            with pe.Fori(2, NG - 1) as g:
                graph_pe(g)
            graph_pe(NG - 1, last=True)
            turn_weights(NG - 1)
            for j in range(GB):
                graph_pv(NG - 1, j)
            pe.wait_ge(on0, B)
            pe.wait_ge(t0m, B)
            pe.wait_ge(s_w2, 16)

            def ln_turn(u, st):
                if not st.on(G_TURN):
                    return
                g, r = st.item(G_TURN), st.mod(G_TURN, 2)
                n = NG * u + g
                pe.wait_ge(xh, GB * (n + 1))
                if st.past(G_TURN + 2):
                    pe.wait_ge(xm, GB * (n - 1))
                for j in range(GB):
                    last = pe.transpose(bank(r, S * j, S * j + S), XH[:, r, j, :], ident[:, :])
                last.then_inc(xt, 1)

            for l in LAYERS:
                u = LN_OF[l.n]

                def project_pe(st):
                    ln_turn(u, st)
                    if not st.on(G_MAIN):
                        return
                    g, r = st.item(G_MAIN), st.mod(G_MAIN, 2)
                    n = NG * l.n + g
                    pe.wait_ge(xm, GB * (NG * u + g + 1))
                    if st.past(G_MAIN + 2):
                        pe.wait_ge(q1, n - 1)
                        pe.wait_ge(kf, n - 1)
                        pe.wait_ge(vc, n - 1)
                    pe.matmul(bank(2 + r), w(l.name + "_q"), XM[:, r, :], start=True, stop=True).then_inc(qp, 1)
                    pe.matmul(bank(4 + r), w(l.name + "_k"), XM[:, r, :], start=True, stop=True).then_inc(kp, 1)
                    for j in range(GB):
                        last = pe.matmul(bank(6 + r, S * j, S * j + S), XM[:, r, S * j:S * j + S], w(l.name + "_v"),
                                         start=True, stop=True)
                    last.then_inc(vp, 1)

                run_steps(pe, project_pe, NG, NG + G_MAIN, 4 if l.n else 6, 2, 2 if l.n else 1)
                pe.wait_ge(xm, GB * NG * (u + 1))
                pe.wait_ge(q1, NG * (l.n + 1))
                pe.wait_ge(kf, NG * (l.n + 1))
                pe.wait_ge(vc, NG * (l.n + 1))

                def attend_pe(st):
                    def score_qk(j):
                        if not st.on(0):
                            return
                        b, v8 = st.item(0), st.mod(0, 8)
                        n = l.banks * b + j
                        if j == 0 and v8 % GB == 0:
                            pe.wait_ge(tl[v8 // GB], TL_BASE[l.n] + 16 * 6 * l.halves * (st.div(0, 8) + 1))
                        if l.n or st.past(1) or j >= 2:
                            pe.wait_ge(mx, S2_BASE[l.n] + n - 1)
                        r, tok = v8 // GB, slice(S * (v8 % GB), S * (v8 % GB) + S)
                        if l.causal:
                            pe.matmul(bank(j % 2), ident_b[:, :], future[:, :, :].rearrange("p h k -> p (h k)"),
                                      start=True, stop=False, skip_group_check=True)
                        for i in range(4):
                            h = 4 * j + i
                            lo = l.half * (h // 8)
                            last = pe.matmul(bank(j % 2, 128 * i, 128 * i + 128), TQ[lo:lo + l.rows, r, h % 8, tok],
                                             TK[lo:lo + l.rows, r, h % 8, tok], start=not l.causal,
                                             stop=(i == 3) if l.causal else True, skip_group_check=l.causal)
                        last.then_inc(s1, 1)

                    def score_kq(j):
                        if not st.on(S_S2):
                            return
                        b, v8 = st.item(S_S2), st.mod(S_S2, 8)
                        n = l.banks * b + j
                        if j == 0:
                            pe.wait_ge(mrow[v8 % 2], MROW_BASE[l.n] + 16 * l.halves * (st.div(S_S2, 2) + 1))
                        if l.n or st.past(S_S2 + 1) or j >= 2:
                            pe.wait_ge(ex, S2_BASE[l.n] + n - 1)
                        r, tok = v8 // GB, slice(S * (v8 % GB), S * (v8 % GB) + S)
                        if l.causal:
                            pe.matmul(bank(2 + j % 2), ident_b[:, :], future_t[:, :, :].rearrange("p h q -> p (h q)"),
                                      start=True, stop=False, skip_group_check=True)
                        for i in range(4):
                            h = 4 * j + i
                            lo = l.half * (h // 8)
                            last = pe.matmul(bank(2 + j % 2, 128 * i, 128 * i + 128),
                                             TK[lo:lo + l.rows + 2, r, h % 8, tok],
                                             TQ[lo:lo + l.rows + 2, r, h % 8, tok], start=not l.causal,
                                             stop=(i == 3) if l.causal else True, skip_group_check=l.causal)
                        last.then_inc(s2, 1)

                    def turn_max():
                        if not st.on(S_MT):
                            return
                        b, r = st.item(S_MT), st.mod(S_MT, 2)
                        m = 16 * l.halves
                        pe.wait_ge(ms2, B * l.n + b + 1)
                        if st.past(S_MT + 1):
                            pe.wait_ge(mtc, B * l.n + b)
                        if st.past(S_OT + 1):
                            pe.wait_ge(otc, B * l.n + (st.item(S_OT) if st.on(S_OT) else B))
                        pe.transpose(P[0:m, 6, 256:320].bitcast(bf16), MB[:, r, 0:m], ident_b[:, :]).then_inc(mt, 1)

                    def turn_o():
                        if not st.on(S_OT):
                            return
                        b, r = st.item(S_OT), st.mod(S_OT, 2)
                        pe.wait_ge(nrm, B * l.n + b + 1)
                        if st.past(S_OT + 1):
                            pe.wait_ge(otc, B * l.n + b)
                        if st.on(S_MT):
                            pe.wait_ge(mtc, B * l.n + st.item(S_MT) + 1)
                        pe.transpose(bank(6, 0, S), ON[:, r, :], ident[:, :]).then_inc(ot, 1)

                    def out_product():
                        if not st.on(S_Y):
                            return
                        b, r = st.item(S_Y), st.mod(S_Y, 2)
                        pe.wait_ge(otc, B * l.n + b + 1)
                        if st.past(S_YT + 1):
                            pe.wait_ge(xadd, B * l.n + b - 1)
                        elif st.past(S_Y + 1):
                            pe.wait_ge(yc, B * l.n + b)
                        pe.matmul(bank(7, 0, S), w(l.name + "_o"), OT[:, r, :], start=True, stop=True).then_inc(yp, 1)

                    def turn_y():
                        if not st.on(S_YT):
                            return
                        b, r = st.item(S_YT), st.mod(S_YT, 2)
                        pe.wait_ge(yc, B * l.n + b + (2 if st.on(S_Y) else 1))
                        if not st.on(S_Y) and st.past(S_YT + 1):
                            pe.wait_ge(xadd, B * l.n + b)
                        pe.transpose(bank(7, 0, D), YS[:, r, :], ident[:, :]).then_inc(yt, 1)

                    def product_v():
                        if not st.on(S_PV):
                            return
                        b, r = st.item(S_PV), st.mod(S_PV, 2)
                        pe.wait_ge(ex, S2_BASE[l.n] + l.banks * (b + 1))
                        pe.wait_ge(vst, B * l.n + b + 1)
                        if st.past(S_PV + 1):
                            pe.wait_ge(o4c, B * l.n + b)
                        for h in range(l.heads):
                            i, lo = h // 4, 32 * (h % 4)
                            last = pe.matmul(P[lo:lo + 32, 4, 128 * i:128 * i + 128], VS[:, r, h, :],
                                             PROB[:, r, h, :], start=True, stop=True,
                                             tile_position=(0, lo))
                        last.then_inc(pv, 1)

                    def turn_heads():
                        if not st.on(S_NR):
                            return
                        b = st.item(S_NR)
                        pe.wait_ge(o4c, B * l.n + b + 1)
                        if st.past(S_NR + 1):
                            pe.wait_ge(nrm, B * l.n + b)
                        for i in range(l.banks):
                            last = pe.transpose(bank(5, 128 * i, 128 * i + 128), O4[:, 128 * i:128 * i + 128],
                                                ident[:, :])
                        last.then_inc(o4t, 1)

                    if l.banks == 4:
                        score_qk(0)
                        score_kq(0)
                        turn_max()
                        turn_heads()
                        score_qk(1)
                        score_kq(1)
                        turn_o()
                        score_qk(2)
                        score_kq(2)
                        out_product()
                        score_qk(3)
                        score_kq(3)
                        turn_y()
                    else:
                        score_qk(0)
                        score_kq(0)
                        turn_max()
                        turn_heads()
                        turn_o()
                        score_qk(1)
                        score_kq(1)
                        out_product()
                        turn_y()
                    product_v()

                run_steps(pe, attend_pe, B, B + S_YT, 8, 8, 3)
                pe.wait_ge(xadd, B * (l.n + 1))
                pe.wait_ge(ex, S2_BASE[l.n] + l.banks * B)

                if l.n == 1:
                    def norm_back(st):
                        ln_turn(3, st)
                        if st.on(G_MAIN):
                            g, r = st.item(G_MAIN), st.mod(G_MAIN, 2)
                            pe.wait_ge(xm, GB * (NG * 3 + g + 1))
                            if st.past(G_MAIN + 2):
                                pe.wait_ge(xg, NG + g - 1)
                            for j in range(GB):
                                last = pe.transpose(bank(6 + r, S * j, S * j + S), XM[:, r, S * j:S * j + S],
                                                    ident[:, :])
                            last.then_inc(ygt, 1)

                    run_steps(pe, norm_back, NG, NG + G_MAIN, 4, 2, 2)
                    pe.wait_ge(xg, 2 * NG)
                    continue

                um, li = (1, 0) if l.n == 0 else (5, 1)

                def mlp_pe(st):
                    ln_turn(um, st)
                    if st.on(G_TAIL):
                        g, r = st.item(G_TAIL), st.mod(G_TAIL, 2)
                        pe.wait_ge(yg, GB * (NG * li + g + 1))
                        if st.past(G_TAIL + 2):
                            pe.wait_ge(xg, 2 * NG * li + g - 1)
                        for j in range(GB):
                            last = pe.transpose(bank(6 + r, S * j, S * j + S), YG[:, S * j:S * j + S], ident[:, :])
                        last.then_inc(ygt, 1)
                    if st.on(G_MAIN):
                        g, r = st.item(G_MAIN), st.mod(G_MAIN, 2)
                        n = NG * li + g

                        def up_product(k):
                            if k == 0:
                                pe.wait_ge(xm, GB * (NG * um + g + 1))
                            if li or st.past(G_MAIN + 1) or k >= 2:
                                pe.wait_ge(ge, 4 * n + k - 1)
                            pe.matmul(bank(2 + k % 2), w(f"{l.name}_up{k}"), XM[:, r, :], start=True,
                                      stop=True).then_inc(up, 1)

                        def down_product(k):
                            pe.wait_ge(ge, 4 * n + k + 1)
                            if k == 0 and st.past(G_MAIN + 2):
                                pe.wait_ge(yg, GB * (n - 1))
                            last = pe.matmul(bank(4 + r), w(f"{l.name}_down{k}"), HID[:, r, k, :], start=(k == 0),
                                             stop=(k == 3))
                            if k == 3:
                                last.then_inc(dn, 1)

                        up_product(0)
                        up_product(1)
                        down_product(0)
                        up_product(2)
                        down_product(1)
                        up_product(3)
                        down_product(2)
                        down_product(3)

                run_steps(pe, mlp_pe, NG, NG + G_TAIL, 4 if li else 6, 2, 2 if li else 1)
                pe.wait_ge(xg, NG * (1 if l.n == 0 else 3))


S2_BASE = [0, 4 * B, 8 * B]
MROW_BASE = [0, 16 * 2 * B // 2, 2 * 16 * 2 * B // 2]
TL_BASE = [0, 16 * 12 * NG // 2, 2 * 16 * 12 * NG // 2]
WR_BASE = [0, 16 * 2 * NG // 2, 2 * 16 * 2 * NG // 2]
WR_END = [16 * 2 * NG // 2, 2 * 16 * 2 * NG // 2, 2 * 16 * 2 * NG // 2 + 16 * NG // 2]
YGT_BASE = [0, 2 * NG]
MODV_END = 40


def lay_out(a):
    t = {k: np.asarray(v) for k, v in a.items()}
    perm16 = np.array([(e * 8 + g) * 8 + d for e in range(2) for d in range(8) for g in range(8)])
    perm8 = np.array([g * 16 + d for d in range(16) for g in range(8)])
    m, cl = {}, {}
    ws = t["L0_cond_W_self"]
    m["l0_self_x"], m["l0_self_q"] = ws[:, :D].T, ws[:, D:].T
    cl["l0_self"] = t["L0_cond_b_self"]
    for d in range(2):
        m[f"l0_q{d}"], m[f"l0_k{d}"] = t["L0_cond_Wq"][d].T, t["L0_cond_Wk"][d].T
        m[f"l0_out{d}"] = t["L0_cond_Wout"][d].reshape(D, D).T
        cl[f"l0_q{d}"], cl[f"l0_k{d}"] = t["L0_cond_bq"][d], t["L0_cond_bk"][d]
    p = "L1_cond_"
    for i in range(6):
        m[f"l1_ada{i}"] = t[p + "Wada"][:, D * i:D * i + D]
        cl[f"l1_ada{i}"] = t[p + "bada"][D * i:D * i + D]
    wq = t[p + "Wqkv"]
    m["l1_q"], m["l1_k"], m["l1_v"] = wq[:, 0:D][:, perm16], wq[:, D:2 * D][:, perm16], wq[:, 2 * D:]
    m["l1_o"], cl["l1_o"] = t[p + "Wproj"], t[p + "bproj"]
    for n in ("g1", "be1", "g2", "be2", "b2"):
        cl["l1_" + n] = t[p + n]
    p = "L2_cond_"
    m["l2_gamma"], m["l2_beta"], m["l2_o"] = t[p + "Wg"].T, t[p + "Wb"].T, t[p + "Wp"].T
    cl["l2_gamma"], cl["l2_beta"], cl["l2_o"] = t[p + "bg"], t[p + "bb"], t[p + "bp"]
    cl["l2_ln_g"], cl["l2_ln_b"] = t[p + "ln_g"], t[p + "ln_b"]
    for i, n in enumerate("qkv"):
        wn, bn = t[p + "Wqkv"][i::3], t[p + "bqkv"][i::3]
        if n != "v":
            wn, bn = wn[perm16], bn[perm16]
        m["l2_" + n], cl["l2_" + n] = wn.T, bn
    p = "L3_cond_"
    for i in range(3):
        for s in "mf":
            m[f"l3_{s}{i}"] = t[p + s + "_ada_w"][:, D * i:D * i + D]
            cl[f"l3_{s}{i}"] = t[p + s + "_ada_b"][D * i:D * i + D]
    for i, n in enumerate("qkv"):
        wn, bn = t[p + "in_proj_w"][D * i:D * i + D], t[p + "in_proj_b"][D * i:D * i + D]
        if n != "v":
            wn, bn = wn[perm8], bn[perm8]
        m["l3_" + n], cl["l3_" + n] = wn.T, bn
    m["l3_o"], cl["l3_o"] = t[p + "out_proj_w"].T, t[p + "out_proj_b"]
    cl["l3_g1"], cl["l3_be1"], cl["l3_g2"], cl["l3_be2"] = (t[p + "m_norm_g"], t[p + "m_norm_b"],
                                                        t[p + "f_norm_g"], t[p + "f_norm_b"])
    cl["l3_b2"] = t[p + "b2"]
    for ly, w1, w2, b1 in (("l1", "L1_cond_W1", "L1_cond_W2", "L1_cond_b1"),
                           ("l3", "L3_cond_w1", "L3_cond_w2", "L3_cond_b1")):
        for k in range(4):
            m[f"{ly}_up{k}"] = t[w1][:, D * k:D * k + D]
            m[f"{ly}_down{k}"] = t[w2][D * k:D * k + D, :]
            cl[f"{ly}_b1_{k}"] = t[b1][D * k:D * k + D]
    mats = np.ascontiguousarray(np.stack([m[n] for n in MATS]))
    cols = np.ascontiguousarray(np.stack([cl[n] for n in COLS], axis=1))
    rows = np.concatenate([t["L0_cond_w_bias"].reshape(-1), t["L0_cond_b_bias"].reshape(-1),
                           t["L0_cond_bout"].reshape(-1)])
    return {"x": t["x"], "cond": t["cond_1024"], "adj": t["mask_BxSxSx11_ik0"], "mats": mats, "cols": cols,
            "rows": rows}


def kernel(**inputs):
    import concourse.bacc as bacc
    from concourse.bass_utils import run_bass_kernel_spmd

    nc = bacc.Bacc("TRN2", target_bir_lowering=False, num_devices=1)
    arrays, args = {}, []
    for name, a in lay_out(inputs).items():
        a = np.ascontiguousarray(a)
        arrays[f"in_{name}"] = a
        args.append(nc.dram_tensor(f"in_{name}", a.shape, mybir.dt.from_np(a.dtype), kind="ExternalInput").ap())
    out = nc.dram_tensor("out_x", (B, S, D), mybir.dt.float32, kind="ExternalOutput").ap()
    build(nc, *args, out)
    r = run_bass_kernel_spmd(nc, [arrays], core_ids=[0])
    return r.results[0]["out_x"]
```
